# Optimizing a Trainium2 kernel written in Bass

```python
import numpy as np
import jax
import jax.numpy as jnp

def _softmax(x, axis=-1):
    return jax.nn.softmax(x, axis=axis)

def _gelu(x):
    return jax.nn.gelu(x, approximate=True)

def _silu(x):
    return jax.nn.silu(x)

def _sigmoid(x):
    return jax.nn.sigmoid(x)

def _layernorm(x, axis=-1, eps=1e-05):
    m = jnp.mean(x, axis=axis, keepdims=True)
    v = jnp.var(x, axis=axis, keepdims=True)
    return (x - m) / jnp.sqrt(v + eps)

def _scatter_add(tgt, idx, src, axis=0):
    return tgt.at[idx].add(src)

def _segment_sum(src, seg, n):
    return jax.ops.segment_sum(src, seg, n)
kernel_name = 'mk_decoder_preln_d4_seqx_r8_e7a077'

def setup_inputs(seed: int=0):
    np.random.seed(seed)
    _w = jnp.asarray

    def _rec_inputs():
        import jax
        import jax.numpy as jnp
        _rk = jax.random.key(seed)
        x = 7.22e-05 + 1 * jax.random.normal(jax.random.fold_in(_rk, 1), (8, 256, 128), jnp.float32)
        _lenS = 256 - jax.random.randint(jax.random.fold_in(_rk, 7), (8,), 0, max(1, 256 // 4) + 1, jnp.int32)
        _lenS2 = 256 - jax.random.randint(jax.random.fold_in(_rk, 8), (8,), 0, max(1, 256 // 4) + 1, jnp.int32)
        _ctx_1024P = jax.random.normal(jax.random.fold_in(_rk, 11), (8, 16, 128), jnp.float32)
        _ctx_1024c = jax.random.dirichlet(jax.random.fold_in(_rk, 511), 0.3 * jnp.ones((16,), jnp.float32), (8, 256))
        _ctx_1024t = jnp.einsum('bsk,bkd->bsd', _ctx_1024c, _ctx_1024P)
        _ctx_1024t = _ctx_1024t * jax.lax.rsqrt(jnp.mean(jnp.square(_ctx_1024t)) + 1e-12) * 0.953939
        ctx_1024 = 4.13588e-05 + 0.999923 * (_ctx_1024t + 0.3 * jax.random.normal(jax.random.fold_in(_rk, 611), (8, 256, 128), jnp.float32))
        _validS = jnp.arange(256)[None, :] < _lenS[:, None]
        _validS2 = jnp.arange(256)[None, :] < _lenS2[:, None]
        _causal = jnp.tril(jnp.ones((256, 256), dtype=bool))
        mask_Bx1xSxS2_ff0 = jnp.where(jnp.ones((8, 1, 256, 256), dtype=bool), 0.0, -1000000000.0).astype(jnp.float32)
        return (x, ctx_1024, mask_Bx1xSxS2_ff0)
    x, ctx_1024, mask_Bx1xSxS2_ff0 = _rec_inputs()

    def _L0_attn_setup():
        import jax, jax.numpy as jnp
        import numpy as np
        B, T, C, H = (2, 256, 128, 16)
        R = 32
        LORA_SCALE = 0.5
        HD = C // H

        def lora_linear(x, w, b, la, lb):
            return x @ w.T + b + LORA_SCALE * (x @ la.T @ lb.T)
        key = jax.random.key(seed)
        ks = jax.random.split(key, 8)
        std = 0.02
        return {'x': jax.random.normal(ks[0], (B, T, C), jnp.float32), 'w_attn': jax.random.normal(ks[1], (3 * C, C), jnp.float32) * std, 'b_attn': jnp.zeros((3 * C,), jnp.float32), 'la_attn': jax.random.normal(ks[2], (R, C), jnp.float32) * std, 'lb_attn': jax.random.normal(ks[3], (3 * C, R), jnp.float32) * std, 'w_proj': jax.random.normal(ks[4], (C, C), jnp.float32) * std, 'b_proj': jnp.zeros((C,), jnp.float32), 'la_proj': jax.random.normal(ks[5], (R, C), jnp.float32) * std, 'lb_proj': jax.random.normal(ks[6], (C, R), jnp.float32) * std}
    _L0_attn_all = _L0_attn_setup()
    _L0_attn_in = {k: v for k, v in _L0_attn_all.items() if k in ('w_attn', 'b_attn', 'la_attn', 'lb_attn', 'w_proj', 'b_proj', 'la_proj', 'lb_proj')}
    del _L0_attn_all

    def _L0_xattn_setup():
        import jax, jax.numpy as jnp
        import numpy as np
        NUM_HEADS = 16

        def trinity_mask(txt_tok, img_tok):
            assert img_tok % 3 == 0, 'Invalid text token sizes'
            sit = img_tok // 3
            N = txt_tok + img_tok
            i = jnp.arange(N)[:, None]
            j = jnp.arange(N)[None, :]
            img_img = (i < img_tok) & (j < img_tok) & (i // sit == j // sit)
            txt_img = (i >= img_tok) & (j < img_tok)
            txt_txt = (i >= img_tok) & (j >= img_tok) & (i >= j)
            return img_img | txt_img | txt_txt
        key = jax.random.key(seed)
        ks = jax.random.split(key, 12)
        B, TXT, IMG = (4, 64, 192)
        N = TXT + IMG
        DQ, DKV = (128, 128)
        s = lambda d: 1.0 / np.sqrt(d).astype(np.float32)
        return {'q': jax.random.normal(ks[0], (B, N, DQ), jnp.float32), 'kv': jax.random.normal(ks[1], (B, N, DKV), jnp.float32), 'Wq': jax.random.normal(ks[2], (DQ, DQ), jnp.float32) * s(DQ), 'bq': jnp.zeros((DQ,), jnp.float32), 'Wk': jax.random.normal(ks[3], (DKV, DQ), jnp.float32) * s(DKV), 'bk': jnp.zeros((DQ,), jnp.float32), 'Wv': jax.random.normal(ks[4], (DKV, DQ), jnp.float32) * s(DKV), 'bv': jnp.zeros((DQ,), jnp.float32), 'Wo': jax.random.normal(ks[5], (DQ, DQ), jnp.float32) * s(DQ), 'bo': jnp.zeros((DQ,), jnp.float32), 'txt_tok_len': TXT, 'img_tok_len': IMG}
    _L0_xattn_all = _L0_xattn_setup()
    _L0_xattn_in = {k: v for k, v in _L0_xattn_all.items() if k in ('Wq', 'bq', 'Wk', 'bk', 'Wv', 'bv', 'Wo', 'bo')}
    del _L0_xattn_all

    def _L0_ffn_setup():
        import jax, jax.numpy as jnp
        import numpy as np
        DIM = 128
        HIDDEN = 384
        SCALE = 1.0 / 127.0

        def _dequant(w_int, dtype):
            return w_int.astype(dtype) * jnp.asarray(SCALE, dtype)
        key = jax.random.key(seed)
        k_x, k_g, k_u, k_d = jax.random.split(key, 4)
        x = jax.random.normal(k_x, (4, 256, DIM), dtype=jnp.float32)
        w_gate = jax.random.randint(k_g, (HIDDEN, DIM), -127, 128, dtype=jnp.int32)
        w_up = jax.random.randint(k_u, (HIDDEN, DIM), -127, 128, dtype=jnp.int32)
        w_down = jax.random.randint(k_d, (DIM, HIDDEN), -127, 128, dtype=jnp.int32)
        return {'x': x, 'w_gate': w_gate, 'w_up': w_up, 'w_down': w_down}
    _L0_ffn_all = _L0_ffn_setup()
    _L0_ffn_in = {k: v for k, v in _L0_ffn_all.items() if k in ('w_gate', 'w_up', 'w_down')}
    del _L0_ffn_all

    def _L1_attn_setup():
        import jax, jax.numpy as jnp
        import numpy as np
        NUM_HEADS = 16

        def _sb_attention(x, Wq, Wk, Wv, Wo):
            b, n, e = x.shape
            h = NUM_HEADS
            d = e // h
            q = (x @ Wq.T).reshape(b, n, h, d).transpose(0, 2, 1, 3)
            k = (x @ Wk.T).reshape(b, n, h, d).transpose(0, 2, 1, 3)
            v = (x @ Wv.T).reshape(b, n, h, d).transpose(0, 2, 1, 3)
            scale = d ** (-0.5)
            logits = jnp.einsum('bhid,bhjd->bhij', q, k) * scale
            mask = jnp.triu(jnp.ones((n, n), dtype=bool), 0)
            log_z = jnp.where(mask, jnp.float32(-100000.0), jax.nn.log_sigmoid(logits))
            log_beta = jnp.where(mask, jnp.float32(0.0), jax.nn.log_sigmoid(-logits))
            total = jnp.sum(log_beta, axis=-1, keepdims=True)
            re_cum_log_beta = total - jnp.cumsum(log_beta, axis=-1)
            att = jnp.exp(log_z + re_cum_log_beta)
            o = jnp.einsum('bhij,bhjd->bhid', att, v)
            rem = 1.0 - jnp.sum(att, axis=-1)
            o = o + rem[..., None] * v
            o = o.transpose(0, 2, 1, 3).reshape(b, n, e)
            return o @ Wo.T
        key = jax.random.key(seed)
        ks = jax.random.split(key, 5)
        b, n, e = (1, 256, 128)
        std = 0.02
        x = jax.random.normal(ks[0], (b, n, e), dtype=jnp.float32)
        Wq = jax.random.normal(ks[1], (e, e), dtype=jnp.float32) * std
        Wk = jax.random.normal(ks[2], (e, e), dtype=jnp.float32) * std
        Wv = jax.random.normal(ks[3], (e, e), dtype=jnp.float32) * std
        Wo = jax.random.normal(ks[4], (e, e), dtype=jnp.float32) * std
        return {'x': x, 'Wq': Wq, 'Wk': Wk, 'Wv': Wv, 'Wo': Wo}
    _L1_attn_all = _L1_attn_setup()
    _L1_attn_in = {k: v for k, v in _L1_attn_all.items() if k in ('Wq', 'Wk', 'Wv', 'Wo')}
    del _L1_attn_all

    def _L1_xattn_setup():
        import jax, jax.numpy as jnp
        import numpy as np
        import math
        D_MODEL = 128
        GNOSIS_DIM = 64
        B, S = (4, 256)
        key = jax.random.key(seed)
        ks = jax.random.split(key, 12)
        s_in = 1.0 / math.sqrt(D_MODEL)
        s_g = 1.0 / math.sqrt(GNOSIS_DIM)
        return {'query': jax.random.normal(ks[0], (B, S, D_MODEL), jnp.float32), 'key': jax.random.normal(ks[1], (B, S, D_MODEL), jnp.float32), 'value': jax.random.normal(ks[2], (B, S, D_MODEL), jnp.float32), 'Wgq': jax.random.normal(ks[3], (GNOSIS_DIM, D_MODEL), jnp.float32) * s_in, 'bgq': jnp.zeros((GNOSIS_DIM,), jnp.float32), 'Wgk': jax.random.normal(ks[4], (GNOSIS_DIM, D_MODEL), jnp.float32) * s_in, 'bgk': jnp.zeros((GNOSIS_DIM,), jnp.float32), 'w_gate': jax.random.normal(ks[5], (), jnp.float32) * s_g, 'b_gate': jnp.zeros((), jnp.float32), 'Wh': jax.random.normal(ks[6], (D_MODEL, D_MODEL), jnp.float32) * s_in, 'bh': jnp.zeros((D_MODEL,), jnp.float32)}
    _L1_xattn_all = _L1_xattn_setup()
    _L1_xattn_in = {k: v for k, v in _L1_xattn_all.items() if k in ('Wgq', 'bgq', 'Wgk', 'bgk', 'w_gate', 'b_gate', 'Wh', 'bh')}
    del _L1_xattn_all

    def _L1_ffn_setup():
        import jax, jax.numpy as jnp
        import numpy as np
        NUM_EXPERTS = 8
        EXPERT_CAPACITY = 2.0
        DIM = 128
        HIDDEN_DIM = 512
        key = jax.random.key(seed)
        k_x, k_g, k_w1, k_w2 = jax.random.split(key, 4)
        n, t, d, f, e = (8, 128, DIM, HIDDEN_DIM, NUM_EXPERTS)
        x = jax.random.normal(k_x, (n, t, d), dtype=jnp.float32)
        gate_w = jax.random.normal(k_g, (e, d), dtype=jnp.float32) * 0.02
        w1 = jax.random.normal(k_w1, (e, d, f), dtype=jnp.float32) * 0.02
        w2 = jax.random.normal(k_w2, (e, f, d), dtype=jnp.float32) * 0.02
        return {'x': x, 'gate_w': gate_w, 'w1': w1, 'w2': w2}
    _L1_ffn_all = _L1_ffn_setup()
    _L1_ffn_in = {k: v for k, v in _L1_ffn_all.items() if k in ('gate_w', 'w1', 'w2')}
    del _L1_ffn_all

    def _L2_attn_setup():
        import jax, jax.numpy as jnp
        import numpy as np
        D_MODEL = 128
        N_HEADS = 16
        HEAD_DIM = D_MODEL // N_HEADS
        ROPE_BASE = 10000.0

        def _rope(q, k):
            S, Dh = (q.shape[1], q.shape[-1])
            inv_freq = 1.0 / ROPE_BASE ** (jnp.arange(0, Dh, 2, dtype=jnp.float32) / Dh)
            t = jnp.arange(S, dtype=jnp.float32)
            freqs = jnp.outer(t, inv_freq)
            emb = jnp.concatenate([freqs, freqs], axis=-1)
            cos = jnp.cos(emb)[None, :, None, :]
            sin = jnp.sin(emb)[None, :, None, :]

            def rotate_half(v):
                v1, v2 = (v[..., :Dh // 2], v[..., Dh // 2:])
                return jnp.concatenate([-v2, v1], axis=-1)
            return (q * cos + rotate_half(q) * sin, k * cos + rotate_half(k) * sin)
        key = jax.random.key(seed)
        ks = jax.random.split(key, 5)
        B, S = (1, 512)
        scale = 1.0 / np.sqrt(D_MODEL)
        x = jax.random.normal(ks[0], (B, S, D_MODEL), dtype=jnp.float32)
        Wq = jax.random.normal(ks[1], (D_MODEL, D_MODEL), dtype=jnp.float32) * scale
        Wk = jax.random.normal(ks[2], (D_MODEL, D_MODEL), dtype=jnp.float32) * scale
        Wv = jax.random.normal(ks[3], (D_MODEL, D_MODEL), dtype=jnp.float32) * scale
        Wo = jax.random.normal(ks[4], (D_MODEL, D_MODEL), dtype=jnp.float32) * scale
        return {'x': x, 'Wq': Wq, 'Wk': Wk, 'Wv': Wv, 'Wo': Wo}
    _L2_attn_all = _L2_attn_setup()
    _L2_attn_in = {k: v for k, v in _L2_attn_all.items() if k in ('Wq', 'Wk', 'Wv', 'Wo')}
    del _L2_attn_all

    def _L2_xattn_setup():
        import jax, jax.numpy as jnp
        import numpy as np
        B, S, D = (4, 256, 128)
        key = jax.random.key(seed)
        kq, kk, kv, kwq, kwk, kwv = jax.random.split(key, 6)
        scale = 0.02
        return {'q': jax.random.normal(kq, (B, S, D), jnp.float32), 'k': jax.random.normal(kk, (B, S, D), jnp.float32), 'v': jax.random.normal(kv, (B, S, D), jnp.float32), 'Wq': jax.random.normal(kwq, (D, D), jnp.float32) * scale, 'Wk': jax.random.normal(kwk, (D, D), jnp.float32) * scale, 'Wv': jax.random.normal(kwv, (D, D), jnp.float32) * scale, 'mask': 1}
    _L2_xattn_all = _L2_xattn_setup()
    _L2_xattn_in = {k: v for k, v in _L2_xattn_all.items() if k in ('Wq', 'Wk', 'Wv')}
    del _L2_xattn_all

    def _L2_ffn_setup():
        import jax, jax.numpy as jnp
        import numpy as np
        D_MODEL = 128
        D_FF = 256
        NUM_EXPERTS = 16
        TOP_K = 2
        CAPACITY_FACTOR = 1.25
        BATCH, SEQ = (4, 256)
        key = jax.random.key(seed)
        k0, k1, k2, k3 = jax.random.split(key, 4)
        x = jax.random.normal(k0, (BATCH, SEQ, D_MODEL), jnp.float32)
        gate_w = jax.random.normal(k1, (NUM_EXPERTS, D_MODEL), jnp.float32) / np.float32(np.sqrt(D_MODEL))
        w1 = jax.random.normal(k2, (NUM_EXPERTS, D_MODEL, D_FF), jnp.float32) / np.float32(np.sqrt(D_MODEL))
        w2 = jax.random.normal(k3, (NUM_EXPERTS, D_FF, D_MODEL), jnp.float32) / np.float32(np.sqrt(D_FF))
        return {'x': x, 'gate_w': gate_w, 'w1': w1, 'w2': w2}
    _L2_ffn_all = _L2_ffn_setup()
    _L2_ffn_in = {k: v for k, v in _L2_ffn_all.items() if k in ('gate_w', 'w1', 'w2')}
    del _L2_ffn_all

    def _L3_attn_setup():
        import jax, jax.numpy as jnp
        import numpy as np
        DILATION_RATE = 4
        SEGMENT_SIZE = 64
        key = jax.random.key(seed)
        x = jax.random.normal(key, (4, 1024, 128), dtype=jnp.float32)
        return {'x': x}
    _L3_attn_all = _L3_attn_setup()
    _L3_attn_in = {k: v for k, v in _L3_attn_all.items() if k in ()}
    del _L3_attn_all

    def _L3_xattn_setup():
        import jax, jax.numpy as jnp
        import numpy as np
        HIDDEN = 128
        HEADS = 16
        N, T1, T2 = (2, 256, 256)

        def _split_heads(x):
            n, t, e = x.shape
            return x.reshape(n, t, HEADS, e // HEADS).transpose(0, 2, 1, 3)
        key = jax.random.key(seed)
        k1, k2, k3, k4 = jax.random.split(key, 4)
        q = jax.random.normal(k1, (N, T1, HIDDEN), dtype=jnp.float32)
        encoder_k = jax.random.normal(k2, (N, T2, HIDDEN), dtype=jnp.float32)
        encoder_v = jax.random.normal(k3, (N, T2, HIDDEN), dtype=jnp.float32)
        encoder_attention_mask = jnp.zeros((N, 1, T2, T2), dtype=jnp.float32)
        wo_w = jax.random.normal(k4, (HIDDEN, HIDDEN), dtype=jnp.float32) * (1.0 / np.sqrt(HIDDEN))
        wo_b = jnp.zeros((HIDDEN,), dtype=jnp.float32)
        return {'q': q, 'encoder_k': encoder_k, 'encoder_v': encoder_v, 'encoder_attention_mask': encoder_attention_mask, 'wo_w': wo_w, 'wo_b': wo_b}
    _L3_xattn_all = _L3_xattn_setup()
    _L3_xattn_in = {k: v for k, v in _L3_xattn_all.items() if k in ('wo_w', 'wo_b')}
    del _L3_xattn_all

    def _L3_ffn_setup():
        import jax, jax.numpy as jnp
        import numpy as np
        S, B, D, FF, E = (128, 2, 128, 256, 8)
        key = jax.random.key(seed)
        ks = jax.random.split(key, 8)
        s = 0.02
        return {'hidden_states': jax.random.normal(ks[0], (S, B, D), dtype=jnp.float32), 'router_w': jax.random.normal(ks[1], (E, D), dtype=jnp.float32) * s, 'expert_gate': jax.random.normal(ks[2], (E, D, FF), dtype=jnp.float32) * s, 'expert_up': jax.random.normal(ks[3], (E, D, FF), dtype=jnp.float32) * s, 'expert_down': jax.random.normal(ks[4], (E, FF, D), dtype=jnp.float32) * s, 'shared_gate': jax.random.normal(ks[5], (D, FF), dtype=jnp.float32) * s, 'shared_up': jax.random.normal(ks[6], (D, FF), dtype=jnp.float32) * s, 'shared_down': jax.random.normal(ks[7], (FF, D), dtype=jnp.float32) * s}
    _L3_ffn_all = _L3_ffn_setup()
    _L3_ffn_in = {k: v for k, v in _L3_ffn_all.items() if k in ('router_w', 'expert_gate', 'expert_up', 'expert_down', 'shared_gate', 'shared_up', 'shared_down')}
    del _L3_ffn_all
    return {'x': x, 'ctx_1024': ctx_1024, 'mask_Bx1xSxS2_ff0': mask_Bx1xSxS2_ff0, 'L0_attn_w_attn': _L0_attn_in['w_attn'], 'L0_attn_b_attn': _L0_attn_in['b_attn'], 'L0_attn_la_attn': _L0_attn_in['la_attn'], 'L0_attn_lb_attn': _L0_attn_in['lb_attn'], 'L0_attn_w_proj': _L0_attn_in['w_proj'], 'L0_attn_b_proj': _L0_attn_in['b_proj'], 'L0_attn_la_proj': _L0_attn_in['la_proj'], 'L0_attn_lb_proj': _L0_attn_in['lb_proj'], 'L0_xattn_Wq': _L0_xattn_in['Wq'], 'L0_xattn_bq': _L0_xattn_in['bq'], 'L0_xattn_Wk': _L0_xattn_in['Wk'], 'L0_xattn_bk': _L0_xattn_in['bk'], 'L0_xattn_Wv': _L0_xattn_in['Wv'], 'L0_xattn_bv': _L0_xattn_in['bv'], 'L0_xattn_Wo': _L0_xattn_in['Wo'], 'L0_xattn_bo': _L0_xattn_in['bo'], 'L0_ffn_w_gate': _L0_ffn_in['w_gate'], 'L0_ffn_w_up': _L0_ffn_in['w_up'], 'L0_ffn_w_down': _L0_ffn_in['w_down'], 'L1_attn_Wq': _L1_attn_in['Wq'], 'L1_attn_Wk': _L1_attn_in['Wk'], 'L1_attn_Wv': _L1_attn_in['Wv'], 'L1_attn_Wo': _L1_attn_in['Wo'], 'L1_xattn_Wgq': _L1_xattn_in['Wgq'], 'L1_xattn_bgq': _L1_xattn_in['bgq'], 'L1_xattn_Wgk': _L1_xattn_in['Wgk'], 'L1_xattn_bgk': _L1_xattn_in['bgk'], 'L1_xattn_w_gate': _L1_xattn_in['w_gate'], 'L1_xattn_b_gate': _L1_xattn_in['b_gate'], 'L1_xattn_Wh': _L1_xattn_in['Wh'], 'L1_xattn_bh': _L1_xattn_in['bh'], 'L1_ffn_gate_w': _L1_ffn_in['gate_w'], 'L1_ffn_w1': _L1_ffn_in['w1'], 'L1_ffn_w2': _L1_ffn_in['w2'], 'L2_attn_Wq': _L2_attn_in['Wq'], 'L2_attn_Wk': _L2_attn_in['Wk'], 'L2_attn_Wv': _L2_attn_in['Wv'], 'L2_attn_Wo': _L2_attn_in['Wo'], 'L2_xattn_Wq': _L2_xattn_in['Wq'], 'L2_xattn_Wk': _L2_xattn_in['Wk'], 'L2_xattn_Wv': _L2_xattn_in['Wv'], 'L2_ffn_gate_w': _L2_ffn_in['gate_w'], 'L2_ffn_w1': _L2_ffn_in['w1'], 'L2_ffn_w2': _L2_ffn_in['w2'], 'L3_xattn_wo_w': _L3_xattn_in['wo_w'], 'L3_xattn_wo_b': _L3_xattn_in['wo_b'], 'L3_ffn_router_w': _L3_ffn_in['router_w'], 'L3_ffn_expert_gate': _L3_ffn_in['expert_gate'], 'L3_ffn_expert_up': _L3_ffn_in['expert_up'], 'L3_ffn_expert_down': _L3_ffn_in['expert_down'], 'L3_ffn_shared_gate': _L3_ffn_in['shared_gate'], 'L3_ffn_shared_up': _L3_ffn_in['shared_up'], 'L3_ffn_shared_down': _L3_ffn_in['shared_down']}

def reference(x, ctx_1024, mask_Bx1xSxS2_ff0, L0_attn_w_attn, L0_attn_b_attn, L0_attn_la_attn, L0_attn_lb_attn, L0_attn_w_proj, L0_attn_b_proj, L0_attn_la_proj, L0_attn_lb_proj, L0_xattn_Wq, L0_xattn_bq, L0_xattn_Wk, L0_xattn_bk, L0_xattn_Wv, L0_xattn_bv, L0_xattn_Wo, L0_xattn_bo, L0_ffn_w_gate, L0_ffn_w_up, L0_ffn_w_down, L1_attn_Wq, L1_attn_Wk, L1_attn_Wv, L1_attn_Wo, L1_xattn_Wgq, L1_xattn_bgq, L1_xattn_Wgk, L1_xattn_bgk, L1_xattn_w_gate, L1_xattn_b_gate, L1_xattn_Wh, L1_xattn_bh, L1_ffn_gate_w, L1_ffn_w1, L1_ffn_w2, L2_attn_Wq, L2_attn_Wk, L2_attn_Wv, L2_attn_Wo, L2_xattn_Wq, L2_xattn_Wk, L2_xattn_Wv, L2_ffn_gate_w, L2_ffn_w1, L2_ffn_w2, L3_xattn_wo_w, L3_xattn_wo_b, L3_ffn_router_w, L3_ffn_expert_gate, L3_ffn_expert_up, L3_ffn_expert_down, L3_ffn_shared_gate, L3_ffn_shared_up, L3_ffn_shared_down):
    import jax
    import jax.numpy as jnp

    def _L0_attn_ref(x, w_attn, b_attn, la_attn, lb_attn, w_proj, b_proj, la_proj, lb_proj):
        import jax, jax.numpy as jnp
        import numpy as np
        B, T, C, H = (2, 256, 128, 16)
        R = 32
        LORA_SCALE = 0.5
        HD = C // H

        def lora_linear(x, w, b, la, lb):
            return x @ w.T + b + LORA_SCALE * (x @ la.T @ lb.T)
        Bsz, Tlen, Cdim = x.shape
        qkv = lora_linear(x, w_attn, b_attn, la_attn, lb_attn)
        q, k, v = jnp.split(qkv, 3, axis=2)
        rs = lambda t: t.reshape(Bsz, Tlen, H, HD).transpose(0, 2, 1, 3)
        q, k, v = (rs(q), rs(k), rs(v))
        att = jnp.einsum('bhqd,bhkd->bhqk', q, k) * (1.0 / np.sqrt(HD))
        causal = jnp.tril(jnp.ones((Tlen, Tlen), dtype=bool))
        att = jnp.where(causal[None, None], att, -jnp.inf)
        att = jax.nn.softmax(att, axis=-1)
        y = jnp.einsum('bhqk,bhkd->bhqd', att, v)
        y = y.transpose(0, 2, 1, 3).reshape(Bsz, Tlen, Cdim)
        return lora_linear(y, w_proj, b_proj, la_proj, lb_proj)

    def _L0_xattn_ref(q, kv, Wq, bq, Wk, bk, Wv, bv, Wo, bo, txt_tok_len, img_tok_len):
        import jax, jax.numpy as jnp
        import numpy as np
        NUM_HEADS = 16

        def trinity_mask(txt_tok, img_tok):
            assert img_tok % 3 == 0, 'Invalid text token sizes'
            sit = img_tok // 3
            N = txt_tok + img_tok
            i = jnp.arange(N)[:, None]
            j = jnp.arange(N)[None, :]
            img_img = (i < img_tok) & (j < img_tok) & (i // sit == j // sit)
            txt_img = (i >= img_tok) & (j < img_tok)
            txt_txt = (i >= img_tok) & (j >= img_tok) & (i >= j)
            return img_img | txt_img | txt_txt
        B, N, C = q.shape
        H = NUM_HEADS
        d = C // H
        scale = d ** (-0.5)
        qh = (q @ Wq + bq).reshape(B, N, H, d).transpose(0, 2, 1, 3)
        kh = (kv @ Wk + bk).reshape(B, N, H, d).transpose(0, 2, 1, 3)
        vh = (kv @ Wv + bv).reshape(B, N, H, d).transpose(0, 2, 1, 3)
        scores = jnp.einsum('bhqd,bhkd->bhqk', qh, kh) * scale
        mask = trinity_mask(txt_tok_len, img_tok_len)
        scores = jnp.where(mask[None, None], scores, -jnp.inf)
        attn = jax.nn.softmax(scores, axis=-1)
        out = jnp.einsum('bhqk,bhkd->bhqd', attn, vh)
        out = out.transpose(0, 2, 1, 3).reshape(B, N, C)
        return out @ Wo + bo

    def _L0_ffn_ref(x, w_gate, w_up, w_down):
        import jax, jax.numpy as jnp
        import numpy as np
        DIM = 128
        HIDDEN = 384
        SCALE = 1.0 / 127.0

        def _dequant(w_int, dtype):
            return w_int.astype(dtype) * jnp.asarray(SCALE, dtype)
        wg = _dequant(w_gate, x.dtype)
        wu = _dequant(w_up, x.dtype)
        wd = _dequant(w_down, x.dtype)
        gate = jnp.einsum('bsd,hd->bsh', x, wg)
        up = jnp.einsum('bsd,hd->bsh', x, wu)
        h = jax.nn.silu(gate) * up
        return jnp.einsum('bsh,dh->bsd', h, wd)

    def _L1_attn_ref(x, Wq, Wk, Wv, Wo):
        import jax, jax.numpy as jnp
        import numpy as np
        NUM_HEADS = 16

        def _sb_attention(x, Wq, Wk, Wv, Wo):
            b, n, e = x.shape
            h = NUM_HEADS
            d = e // h
            q = (x @ Wq.T).reshape(b, n, h, d).transpose(0, 2, 1, 3)
            k = (x @ Wk.T).reshape(b, n, h, d).transpose(0, 2, 1, 3)
            v = (x @ Wv.T).reshape(b, n, h, d).transpose(0, 2, 1, 3)
            scale = d ** (-0.5)
            logits = jnp.einsum('bhid,bhjd->bhij', q, k) * scale
            mask = jnp.triu(jnp.ones((n, n), dtype=bool), 0)
            log_z = jnp.where(mask, jnp.float32(-100000.0), jax.nn.log_sigmoid(logits))
            log_beta = jnp.where(mask, jnp.float32(0.0), jax.nn.log_sigmoid(-logits))
            total = jnp.sum(log_beta, axis=-1, keepdims=True)
            re_cum_log_beta = total - jnp.cumsum(log_beta, axis=-1)
            att = jnp.exp(log_z + re_cum_log_beta)
            o = jnp.einsum('bhij,bhjd->bhid', att, v)
            rem = 1.0 - jnp.sum(att, axis=-1)
            o = o + rem[..., None] * v
            o = o.transpose(0, 2, 1, 3).reshape(b, n, e)
            return o @ Wo.T
        return _sb_attention(x, Wq, Wk, Wv, Wo)

    def _L1_xattn_ref(query, key, value, Wgq, bgq, Wgk, bgk, w_gate, b_gate, Wh, bh):
        import jax, jax.numpy as jnp
        import numpy as np
        import math
        D_MODEL = 128
        GNOSIS_DIM = 64
        B, S = (4, 256)
        scale = math.sqrt(D_MODEL)
        scores = jnp.einsum('bqd,bkd->bqk', query, key) / scale
        gq = jnp.tanh(jnp.einsum('bqd,gd->bqg', query, Wgq) + bgq)
        gk = jnp.tanh(jnp.einsum('bkd,gd->bkg', key, Wgk) + bgk)
        gnosis_scores = jnp.einsum('bqg,bkg->bqk', gq, gk)
        gnosis_weights = jax.nn.sigmoid(gnosis_scores * w_gate + b_gate)
        scores = scores * (1.0 + gnosis_weights)
        attention = jax.nn.softmax(scores, axis=-1)
        out = jnp.einsum('bqk,bkd->bqd', attention, value)
        out = jnp.einsum('bqd,ed->bqe', out, Wh) + bh
        return out

    def _L1_ffn_ref(x, gate_w, w1, w2):
        import jax, jax.numpy as jnp
        import numpy as np
        NUM_EXPERTS = 8
        EXPERT_CAPACITY = 2.0
        DIM = 128
        HIDDEN_DIM = 512
        n, t, d = x.shape
        e = gate_w.shape[0]
        k = int(EXPERT_CAPACITY * t / e)
        scores = jnp.einsum('ntd,ed->nte', x, gate_w)
        probs = jax.nn.softmax(scores, axis=-1)
        g, m = jax.lax.top_k(probs.transpose(0, 2, 1), k)
        batch_idx = jnp.arange(n)[:, None, None]
        xin = x[batch_idx, m]
        h = jnp.einsum('nekd,edf->nekf', xin, w1)
        h = jax.nn.gelu(h, approximate=False)
        h = jnp.einsum('nekf,efd->nekd', h, w2)
        out_tok = g[..., None] * h
        out = jnp.zeros((n, t, d), dtype=x.dtype).at[batch_idx, m].add(out_tok)
        return out

    def _L2_attn_ref(x, Wq, Wk, Wv, Wo):
        import jax, jax.numpy as jnp
        import numpy as np
        D_MODEL = 128
        N_HEADS = 16
        HEAD_DIM = D_MODEL // N_HEADS
        ROPE_BASE = 10000.0

        def _rope(q, k):
            S, Dh = (q.shape[1], q.shape[-1])
            inv_freq = 1.0 / ROPE_BASE ** (jnp.arange(0, Dh, 2, dtype=jnp.float32) / Dh)
            t = jnp.arange(S, dtype=jnp.float32)
            freqs = jnp.outer(t, inv_freq)
            emb = jnp.concatenate([freqs, freqs], axis=-1)
            cos = jnp.cos(emb)[None, :, None, :]
            sin = jnp.sin(emb)[None, :, None, :]

            def rotate_half(v):
                v1, v2 = (v[..., :Dh // 2], v[..., Dh // 2:])
                return jnp.concatenate([-v2, v1], axis=-1)
            return (q * cos + rotate_half(q) * sin, k * cos + rotate_half(k) * sin)
        B, S, _ = x.shape
        H, Dh = (N_HEADS, HEAD_DIM)
        q = (x @ Wq.T).reshape(B, S, H, Dh)
        k = (x @ Wk.T).reshape(B, S, H, Dh)
        v = (x @ Wv.T).reshape(B, S, H, Dh)
        q, k = _rope(q, k)
        scale = 1.0 / np.sqrt(Dh)
        scores = jnp.einsum('bqhd,bkhd->bhqk', q, k) * scale
        causal = jnp.triu(jnp.ones((S, S), dtype=bool), k=1)
        scores = jnp.where(causal, -jnp.inf, scores)
        attn = jax.nn.softmax(scores, axis=-1)
        out = jnp.einsum('bhqk,bkhd->bqhd', attn, v).reshape(B, S, H * Dh)
        return out @ Wo.T

    def _L2_xattn_ref(q, k, v, Wq, Wk, Wv, mask):
        import jax, jax.numpy as jnp
        import numpy as np
        B, S, D = (4, 256, 128)
        Q = jnp.einsum('bsd,de->bse', q, Wq)
        K = jnp.einsum('bsd,de->bse', k, Wk)
        V = jnp.einsum('bsd,de->bse', v, Wv)
        d_k = Q.shape[-1]
        scores = jnp.einsum('bqd,bkd->bqk', Q, K) / jnp.sqrt(jnp.float32(d_k))
        if mask:
            causal = jnp.triu(jnp.ones((S, S), dtype=bool), k=1)
            scores = jnp.where(causal[None, :, :], -jnp.inf, scores)
        attn = jax.nn.softmax(scores, axis=-1)
        return jnp.einsum('bqk,bkd->bqd', attn, V)

    def _L2_ffn_ref(x, gate_w, w1, w2):
        import jax, jax.numpy as jnp
        import numpy as np
        D_MODEL = 128
        D_FF = 256
        NUM_EXPERTS = 16
        TOP_K = 2
        CAPACITY_FACTOR = 1.25
        BATCH, SEQ = (4, 256)
        B, S, d = x.shape
        T = B * S
        E, K = (NUM_EXPERTS, TOP_K)
        capacity = int(CAPACITY_FACTOR * T * K / E)
        xf = x.reshape(T, d)
        logits = xf @ gate_w.T
        probs = jax.nn.sigmoid(logits)
        top_vals, sel = jax.lax.top_k(probs, K)
        weights = top_vals / (top_vals.sum(-1, keepdims=True) + 1e-06)
        flat_sel = sel.reshape(-1)
        onehot = jax.nn.one_hot(flat_sel, E, dtype=jnp.int32)
        ranks = jnp.take_along_axis(jnp.cumsum(onehot, axis=0), flat_sel[:, None], axis=1)[:, 0] - 1
        valid = ranks < capacity
        sentinel = E * capacity
        slot = jnp.where(valid, flat_sel * capacity + ranks, sentinel)
        x_rep = jnp.repeat(xf, K, axis=0)
        padded = jnp.zeros((sentinel + 1, d), xf.dtype).at[slot].set(x_rep)
        padded = padded[:sentinel].reshape(E, capacity, d)
        h = jax.nn.gelu(jnp.einsum('ecd,edf->ecf', padded, w1), approximate=False)
        out_padded = jnp.einsum('ecf,efd->ecd', h, w2).reshape(sentinel, d)
        gathered = out_padded[jnp.minimum(slot, sentinel - 1)]
        gathered = jnp.where(valid[:, None], gathered, jnp.zeros((), xf.dtype))
        out = (gathered * weights.reshape(-1)[:, None]).reshape(T, K, d).sum(axis=1)
        return out.reshape(B, S, d)

    def _L3_attn_ref(x):
        import jax, jax.numpy as jnp
        import numpy as np
        DILATION_RATE = 4
        SEGMENT_SIZE = 64
        'LongNet-style dilated attention.\n\n            For each offset in range(dilation_rate): take the strided slice\n            x[:, offset::r, :], split it into segments of length `segment_size`,\n            run full softmax(q k^T / sqrt(d)) v attention inside each segment\n            (q=k=v=the slice; attention dim is the full d_model, matching how the\n            original feeds [B, n_seg, seg, d_model] to FlashAttention), scatter the\n            result back to the strided positions, and average the dilation heads\n            (softmax over uniform logits == 1/r weights).\n\n            Since seq_len % (r * segment_size) == 0, the r strided slices tile the\n            sequence exactly, so we vectorize over offsets with a single reshape:\n            position p = i*r + offset  ->  xr[:, i, offset, :].\n            '
        r, seg = (DILATION_RATE, SEGMENT_SIZE)
        B, S, D = x.shape
        n = S // r
        g = n // seg
        scale = 1.0 / jnp.sqrt(jnp.asarray(D, dtype=x.dtype))
        xs = x.reshape(B, g, seg, r, D)
        scores = jnp.einsum('bgqrd,bgkrd->brgqk', xs, xs) * scale
        probs = jax.nn.softmax(scores, axis=-1)
        out = jnp.einsum('brgqk,bgkrd->bgqrd', probs, xs)
        return out.reshape(B, S, D) / r

    def _L3_xattn_ref(q, encoder_k, encoder_v, encoder_attention_mask, wo_w, wo_b):
        import jax, jax.numpy as jnp
        import numpy as np
        HIDDEN = 128
        HEADS = 16
        N, T1, T2 = (2, 256, 256)

        def _split_heads(x):
            n, t, e = x.shape
            return x.reshape(n, t, HEADS, e // HEADS).transpose(0, 2, 1, 3)
        qh = _split_heads(q)
        kh = _split_heads(encoder_k)
        vh = _split_heads(encoder_v)
        scores = jnp.einsum('bhqd,bhkd->bhqk', qh, kh) + encoder_attention_mask
        weights = jax.nn.softmax(scores, axis=-1)
        ctx = jnp.einsum('bhqk,bhkd->bhqd', weights, vh)
        ctx = ctx.transpose(0, 2, 1, 3).reshape(q.shape[0], q.shape[1], -1)
        return jax.nn.relu(ctx @ wo_w.T + wo_b)

    def _L3_ffn_ref(hidden_states, router_w, expert_gate, expert_up, expert_down, shared_gate, shared_up, shared_down):
        import jax, jax.numpy as jnp
        import numpy as np
        S, B, D, FF, E = (128, 2, 128, 256, 8)
        seq, bs, d = hidden_states.shape
        n_experts = expert_gate.shape[0]
        x = hidden_states.reshape(-1, d)
        logits = jnp.einsum('td,ed->te', x, router_w)
        top_logit = jnp.max(logits, axis=-1)
        top_idx = jnp.argmax(logits, axis=-1)
        score = jax.nn.sigmoid(top_logit)
        onehot = jax.nn.one_hot(top_idx, n_experts, dtype=x.dtype)
        xs = x * score[:, None]
        g = jnp.einsum('td,edf->etf', xs, expert_gate)
        u = jnp.einsum('td,edf->etf', xs, expert_up)
        h = jax.nn.silu(g) * u
        eo = jnp.einsum('etf,efd->etd', h, expert_down)
        moe_out = jnp.einsum('te,etd->td', onehot, eo)
        sh = jax.nn.silu(x @ shared_gate) * (x @ shared_up) @ shared_down
        return (moe_out + sh).reshape(seq, bs, d)
    x = x + _L0_attn_ref(_layernorm(x, axis=-1), L0_attn_w_attn, L0_attn_b_attn, L0_attn_la_attn, L0_attn_lb_attn, L0_attn_w_proj, L0_attn_b_proj, L0_attn_la_proj, L0_attn_lb_proj)
    x = x + _L0_xattn_ref(_layernorm(x, axis=-1), ctx_1024, L0_xattn_Wq, L0_xattn_bq, L0_xattn_Wk, L0_xattn_bk, L0_xattn_Wv, L0_xattn_bv, L0_xattn_Wo, L0_xattn_bo, 64, 192)
    x = x + _L0_ffn_ref(_layernorm(x, axis=-1), L0_ffn_w_gate, L0_ffn_w_up, L0_ffn_w_down)
    x = x + _L1_attn_ref(_layernorm(x, axis=-1), L1_attn_Wq, L1_attn_Wk, L1_attn_Wv, L1_attn_Wo)
    x = x + _L1_xattn_ref(_layernorm(x, axis=-1), ctx_1024, ctx_1024, L1_xattn_Wgq, L1_xattn_bgq, L1_xattn_Wgk, L1_xattn_bgk, L1_xattn_w_gate, L1_xattn_b_gate, L1_xattn_Wh, L1_xattn_bh)
    x = x + _L1_ffn_ref(_layernorm(x, axis=-1), L1_ffn_gate_w, L1_ffn_w1, L1_ffn_w2)
    x = x + _L2_attn_ref(_layernorm(x, axis=-1), L2_attn_Wq, L2_attn_Wk, L2_attn_Wv, L2_attn_Wo)
    x = x + _L2_xattn_ref(_layernorm(x, axis=-1), ctx_1024, ctx_1024, L2_xattn_Wq, L2_xattn_Wk, L2_xattn_Wv, 1)
    x = x + _L2_ffn_ref(_layernorm(x, axis=-1), L2_ffn_gate_w, L2_ffn_w1, L2_ffn_w2)
    x = x + _L3_attn_ref(_layernorm(x, axis=-1))
    x = x + _L3_xattn_ref(_layernorm(x, axis=-1), ctx_1024, ctx_1024, mask_Bx1xSxS2_ff0, L3_xattn_wo_w, L3_xattn_wo_b)
    x = x + _L3_ffn_ref(_layernorm(x, axis=-1), L3_ffn_router_w, L3_ffn_expert_gate, L3_ffn_expert_up, L3_ffn_expert_down, L3_ffn_shared_gate, L3_ffn_shared_up, L3_ffn_shared_down)
    return x

_drawn_inputs = setup_inputs


def setup_inputs(seed=0):
    import zlib

    import numpy as np

    out = dict(_drawn_inputs(seed))
    spreads = {'L0_attn_b_attn': (0.0, 0.308),
     'L0_attn_b_proj': (0.0, 0.1),
     'L0_xattn_bq': (0.0, 0.1),
     'L0_xattn_bk': (0.0, 2.0),
     'L0_xattn_bv': (0.0, 0.1),
     'L0_xattn_bo': (0.0, 0.1),
     'L1_xattn_bgq': (0.0, 2.0),
     'L1_xattn_bgk': (0.0, 2.0),
     'L1_xattn_bh': (0.0, 2.0),
     'L3_xattn_wo_b': (0.0, 2.0)}
    factors = {'L0_attn_w_attn': 5.702,
     'L0_attn_la_attn': 8.0,
     'L0_attn_lb_attn': 8.0,
     'L0_attn_la_proj': 8.0,
     'L0_attn_lb_proj': 8.0,
     'L1_attn_Wq': 33.998,
     'L1_attn_Wk': 35.799,
     'L1_attn_Wv': 23.798,
     'L1_attn_Wo': 22.664,
     'L1_xattn_Wgq': 64.0,
     'L1_xattn_Wgk': 64.0,
     'L1_xattn_Wh': 8.0,
     'L1_ffn_gate_w': 23.865,
     'L1_ffn_w1': 25.313,
     'L1_ffn_w2': 22.874,
     'L2_attn_Wq': 8.0,
     'L2_attn_Wk': 8.0,
     'L2_attn_Wv': 8.0,
     'L2_attn_Wo': 8.0,
     'L2_xattn_Wq': 57.995,
     'L2_xattn_Wk': 60.675,
     'L2_xattn_Wv': 52.57,
     'L2_ffn_gate_w': 8.0,
     'L2_ffn_w1': 8.0,
     'L2_ffn_w2': 8.0,
     'L3_xattn_wo_w': 32.561,
     'L3_ffn_router_w': 36.071,
     'L3_ffn_expert_gate': 38.147,
     'L3_ffn_expert_up': 34.47,
     'L3_ffn_expert_down': 34.238,
     'L3_ffn_shared_gate': 32.486,
     'L3_ffn_shared_up': 28.945,
     'L3_ffn_shared_down': 29.253}
    for name, (base, spread) in spreads.items():
        noise = np.random.default_rng([zlib.crc32(name.encode()), seed]).standard_normal(out[name].shape)
        drawn = base * np.exp(spread * noise) if base else spread * noise
        out[name] = jnp.asarray(drawn.astype(out[name].dtype))
    for name, factor in factors.items():
        out[name] = (out[name] * factor).astype(out[name].dtype)
    return out
```

```python
from contextlib import ExitStack

import numpy as np
import concourse.bass as bass
from concourse import mybir

F32 = mybir.dt.float32
BF16 = mybir.dt.bfloat16
I32 = mybir.dt.int32
ALU = mybir.AluOpType
ACT = mybir.ActivationFunctionType
AX = mybir.AxisListType

P = 128
B, S, D = 8, 256, 128
TPB = S // P
NT = B * TPB
H, HD = 16, 8
VW = HD + 1
BIG = -1.0e30
LEAST = -3.0e38
EPS = 1e-5


class Count:

    def __init__(self, sem, n):
        self.sem, self.n = sem, n

    def credit(self, eng):
        eng.sem_inc(self.sem, self.n)

    def now(self, b, k):
        return b * self.n + (self.n + k)

    def before(self, b, k):
        return b * self.n + k


class Chain:

    def __init__(self, eng, count):
        self.eng, self.count, self.k, self.b = eng, count, 0, 0

    def batch(self, b):
        self.b, self.k = b, 0

    def step(self, ins):
        ins.then_inc(self.count.sem, 1)
        self.k += 1
        self.eng.wait_ge(self.count.sem, self.count.now(self.b, self.k))

    def done(self):
        assert self.k == self.count.n, (self.k, self.count.n)


class Semaphores:

    def __init__(self, nc):
        self.nc, self.held = nc, []

    def __call__(self, name):
        self.held.append(self.nc.alloc_semaphore(name))
        return self.held[-1]

    def __enter__(self):
        return self

    def __exit__(self, *why):
        if why[0] is None:
            self.nc.clear_and_free_semaphores(self.held)
            self.nc.all_engine_barrier()


class Mem:

    def __init__(self, nc, ctx):
        def sb(name, shape, dt=F32):
            return ctx.enter_context(nc.sbuf_tensor(name, shape, dt))

        self.x = sb("x_resid", [P, NT, D])
        self.ctx = sb("ctx_nat", [P, NT, D])
        self.ctxT = sb("ctx_T", [P, NT * P])
        self.stats = sb("bn_stats", [P, TPB, 6])
        self.agg = sb("bn_aggr", [P, TPB, 2])
        self.mv = sb("mean_var", [P, NT, 2])
        self.rstd = sb("rstd", [P, NT])
        self.lnv = sb("ln_var", [P, NT])
        self.eps = sb("eps_col", [P, 1])
        self.ident = sb("ident", [P, P])
        self.identb = sb("identb", [P, P], BF16)
        self.ones_row = sb("ones_row", [1, S])
        self.bias = sb("bias_rows", [1, 16, P])
        self.settled = ctx.enter_context(nc.semaphore("settled"))

    def settle(self, eng):
        eng.sem_inc(self.settled, 1)


def layernorm_scales(nc, mem, name, sem):
    with nc.Block() as block:
        @block.scalar
        def _(act):
            act.preload_act_table_set("natural_log_exp_and_others")
            nc.scalar.activation(mem.lnv[:], mem.mv[:, :, 1], ACT.Ln, bias=mem.eps[:]).then_inc(sem, 1)
            act.wait_ge(sem, 1)
            nc.scalar.activation(mem.rstd[:], mem.lnv[:], ACT.Exp, scale=-0.5).then_inc(sem, 1)


def tile2(mem_tile, b):
    return mem_tile[:, bass.ds(b * TPB, TPB), :]


def normalize(nc, mem, dve, chain, b, h):
    mean = mem.mv[:, bass.ds(b * TPB, TPB), 0:1].to_broadcast([P, TPB, D])
    rstd = mem.rstd[:, bass.ds(b * TPB, TPB)].unsqueeze(2).to_broadcast([P, TPB, D])
    chain.step(nc.vector.tensor_tensor(h[:], tile2(mem.x, b), mean, ALU.subtract))
    return nc.vector.tensor_tensor(h[:], h[:], rstd, ALU.mult)


def take_stats(nc, mem, dve, chain, b):
    for t in range(TPB):
        chain.step(nc.vector.bn_stats(mem.stats[:, t, :], mem.x[:, bass.ds(b * TPB + t, 1), :]))
        mem.settle(dve)
        chain.step(nc.vector.bn_aggr(mem.agg[:, t, :], mem.stats[:, t, :]))
        mem.settle(dve)
    chain.step(nc.vector.tensor_copy(mem.mv[:, bass.ds(b * TPB, TPB), :], mem.agg[:]))


def each_batch(eng, batch):
    with eng.Fori(0, B - 1) as b:
        batch(b, False)
    batch(B - 1, True)


SQUARE = ["L1_attn_Wq", "L1_attn_Wk", "L1_attn_Wv", "L1_attn_Wo", "L1_xattn_Wh",
          "L2_attn_Wq", "L2_attn_Wk", "L2_attn_Wv", "L2_attn_Wo", "L3_xattn_wo_w", "L0_attn_w_proj"]
DIRECT = ["L0_xattn_Wq", "L0_xattn_Wk", "L0_xattn_Wv", "L0_xattn_Wo",
          "L2_xattn_Wq", "L2_xattn_Wk", "L2_xattn_Wv"]
BIASES = {"L0_attn_b_attn": 0, "L0_attn_b_proj": 3, "L0_xattn_bq": 4, "L0_xattn_bk": 5, "L0_xattn_bv": 6,
          "L0_xattn_bo": 7, "L1_xattn_bh": 8, "L3_xattn_wo_b": 9}
RANK = 32
LORA_SCALE = 0.5
HID0 = 384
GN = 64


def load_and_turn(nc, mem, w, dram):
    with ExitStack() as ctx:
        sems = ctx.enter_context(Semaphores(nc))

        def sb(name, shape, dt=F32):
            return ctx.enter_context(nc.sbuf_tensor(name, shape, dt))

        def sem(name):
            return sems(name)

        nat = {n: sb("nat_" + n, [P, P]) for n in SQUARE}
        w_attn = sb("nat_w_attn", [P, 3, P])
        lb_attn = sb("nat_lb_attn", [P, 3, RANK])
        lb_proj = sb("nat_lb_proj", [P, RANK])
        la_attn = sb("nat_la_attn", [RANK, P])
        la_proj = sb("nat_la_proj", [RANK, P])
        lbT_attn = sb("lbT_attn", [RANK, 3 * P])
        lbT_proj = sb("lbT_proj", [RANK, P])
        ffn_int = sb("nat_ffn_int", [P, 3, HID0], I32)
        ffn_nat = sb("nat_ffn", [P, 3, HID0])
        wgq = sb("nat_Wgq", [GN, P])
        wgk = sb("nat_Wgk", [GN, P])
        gates = {"L1_ffn_gate_w": 8, "L2_ffn_gate_w": 16, "L3_ffn_router_w": 8}
        gate_nat = {n: sb("nat_" + n, [e, P]) for n, e in gates.items()}
        rings = 6
        psum = [ctx.enter_context(nc.psum_tensor(f"turn{i}", [P, P], F32)) for i in range(rings)]
        lora = ctx.enter_context(nc.psum_tensor("lora", [P, 4 * P], F32))
        loaded, first, casts = sem("weights_loaded"), sem("x_loaded"), sem("dequantized")
        built, turned, moved_act, moved_dve = sem("ident_built"), sem("turned"), sem("moved_by_act"), sem("moved_by_dve")
        lora_done, chain = sem("lora_done"), sem("prologue_chain")

        turns = [(w_attn[:, j, :], w["L0_attn_w_attn"][:, j * P:(j + 1) * P]) for j in range(3)]
        turns += [(lb_attn[:, j, :], lbT_attn[:, j * P:(j + 1) * P]) for j in range(3)]
        turns += [(lb_proj[:], lbT_proj[:])]
        turns += [(nat[n][:], w[n][:]) for n in SQUARE]
        turns += [(wgq[:], w["L1_xattn_Wgq"][:]), (wgk[:], w["L1_xattn_Wgk"][:])]
        turns += [(gate_nat[n][:], w[n][:]) for n in gates]
        turns += [(mem.ctx[:, t, :], mem.ctxT[:, t * P:(t + 1) * P]) for t in range(NT)]
        from_int = len(turns)
        turns += [(ffn_nat[:, 0, j * P:(j + 1) * P], w["L0_ffn_w_down"][:, j, :]) for j in range(3)]
        turns += [(ffn_nat[:, 1, j * P:(j + 1) * P], w["L0_ffn_w_gate"][:, j * P:(j + 1) * P]) for j in range(3)]
        turns += [(ffn_nat[:, 2, j * P:(j + 1) * P], w["L0_ffn_w_up"][:, j * P:(j + 1) * P]) for j in range(3)]
        lora_after = 7

        def square(n):
            return dram[n]

        firsts = [(mem.x[:], dram["x"].rearrange("b (t p) d -> p (b t) d", p=P))]
        loads = [
            (w_attn[:], dram["L0_attn_w_attn"].rearrange("(j p) d -> p j d", p=P)),
            (lb_attn[:], dram["L0_attn_lb_attn"].rearrange("(j p) r -> p j r", p=P)),
            (lb_proj[:], dram["L0_attn_lb_proj"]), (la_attn[:], dram["L0_attn_la_attn"]),
            (la_proj[:], dram["L0_attn_la_proj"]),
            (mem.ctx[:], dram["ctx_1024"].rearrange("b (t p) d -> p (b t) d", p=P)),
            (ffn_int[:, 0, :], dram["L0_ffn_w_down"]),
            (ffn_int[:, 1, :].rearrange("p (j d) -> p j d", d=P), dram["L0_ffn_w_gate"].rearrange("(j p) d -> p j d", p=P)),
            (ffn_int[:, 2, :].rearrange("p (j d) -> p j d", d=P), dram["L0_ffn_w_up"].rearrange("(j p) d -> p j d", p=P)),
            (wgq[:], dram["L1_xattn_Wgq"]), (wgk[:], dram["L1_xattn_Wgk"]),
            (w["bgq"][:], dram["L1_xattn_bgq"].rearrange("(p a) -> p a", a=1)),
            (w["bgk"][:], dram["L1_xattn_bgk"].rearrange("(p a) -> p a", a=1)),
            (w["rope"][:], dram["rope"]),
            (w["w_gate"][:], dram["L1_xattn_w_gate"].rearrange("(p a) -> p a", a=1).to_broadcast([P, 1])),
            (w["b_gate"][:], dram["L1_xattn_b_gate"].rearrange("(p a) -> p a", a=1).to_broadcast([P, 1])),
        ]
        loads += [(nat[n][:], dram[n]) for n in SQUARE]
        loads += [(w[n][:], dram[n]) for n in DIRECT]
        loads += [(gate_nat[n][:], dram[n]) for n in gates]
        loads += [(mem.bias[0:1, k:k + dram[n].shape[0] // P, :],
                   dram[n].rearrange("(a j p) -> a j p", a=1, p=P)) for n, k in BIASES.items()]
        late = [
            (w["L1_ffn_w1"], dram["L1_ffn_w1"].rearrange("e d f -> d e f")),
            (w["L1_ffn_w2"], dram["L1_ffn_w2"].rearrange("e (c f) d -> f e c d", f=P)),
        ]
        w["late_count"] = 16 * len(late)

        with nc.Block() as block:
            @block.sync
            def _(sp):
                for dst, src in firsts:
                    sp.dma_start(dst, src).then_inc(first, 16)
                for dst, src in loads:
                    sp.dma_start(dst, src).then_inc(loaded, 16)
                for dst, src in late:
                    sp.dma_start(dst, src).then_inc(w["late"], 16)

            @block.gpsimd
            def _(pool):
                steps = Chain(pool, Count(built, 0))
                for dst in (mem.ident, mem.identb):
                    steps.step(nc.gpsimd.memset(dst[:], 0.0))
                    steps.step(nc.gpsimd.affine_select(out=dst[:], in_=dst[:], compare_op=ALU.not_equal, fill=1.0,
                                                       base=0, pattern=[[-1, P]], channel_multiplier=1))
                steps.step(nc.gpsimd.memset(w["causal"][:], 0.0))
                steps.step(nc.gpsimd.affine_select(out=w["causal"][:], in_=w["causal"][:], compare_op=ALU.is_ge,
                                                   fill=BIG, base=0, pattern=[[-1, P]], channel_multiplier=1))
                steps.step(nc.gpsimd.memset(w["strict"][:], 0.0))
                steps.step(nc.gpsimd.affine_select(out=w["strict"][:], in_=w["strict"][:], compare_op=ALU.is_gt,
                                                   fill=BIG, base=0, pattern=[[1, P]], channel_multiplier=-1))
                steps.step(nc.gpsimd.iota(w["offset"][:], pattern=[[1, P]], base=P, channel_multiplier=-1))
                tri = w["trinity"]
                half = P // 2
                steps.step(nc.gpsimd.memset(tri[:], BIG))
                for q in range(3):
                    t, r = divmod(q * half, P)
                    steps.step(nc.gpsimd.memset(tri[r:r + half, t, q * half:(q + 1) * half], 0.0))
                steps.step(nc.gpsimd.memset(tri[half:P, 1, :], 0.0))
                steps.step(nc.gpsimd.affine_select(out=tri[half:P, 1, 3 * half:S], in_=tri[half:P, 1, 3 * half:S],
                                                   compare_op=ALU.is_ge, fill=BIG, base=0, pattern=[[-1, half]],
                                                   channel_multiplier=1))
                for dst in (w["sel"][:],):
                    steps.step(nc.gpsimd.memset(dst, 0.0))
                    for off in (0, 32):
                        steps.step(nc.gpsimd.affine_select(out=dst, in_=dst, compare_op=ALU.not_equal, fill=1.0,
                                                           base=-off, pattern=[[-1, H], [0, P]], channel_multiplier=1))
                steps.step(nc.gpsimd.memset(w["rows"][:], 1.0))
                steps.step(nc.gpsimd.affine_select(out=w["rows"][:], in_=w["rows"][:], compare_op=ALU.is_ge, fill=0.0, base=0,
                                                   pattern=[[-HD, H]], channel_multiplier=1))
                steps.step(nc.gpsimd.affine_select(out=w["rows"][:], in_=w["rows"][:], compare_op=ALU.is_ge, fill=0.0,
                                                   base=HD - 1, pattern=[[HD, H]], channel_multiplier=-1))
                steps.step(nc.gpsimd.memset(w["neg_ones"][:], -1.0))
                steps.step(nc.gpsimd.memset(w["neg_tri"][:], -1.0))
                steps.step(nc.gpsimd.affine_select(out=w["neg_tri"][:], in_=w["neg_tri"][:], compare_op=ALU.is_ge,
                                                   fill=0.0, base=0, pattern=[[-1, P]], channel_multiplier=1))
                steps.step(nc.gpsimd.memset(w["ones"][:], 1.0))
                steps.step(nc.gpsimd.memset(w["earlier"][:], 1.0))
                steps.step(nc.gpsimd.affine_select(out=w["earlier"][:], in_=w["earlier"][:], compare_op=ALU.is_gt,
                                                   fill=0.0, base=0, pattern=[[1, P]], channel_multiplier=-1))
                steps.step(nc.gpsimd.memset(mem.ones_row[:], 1.0))
                steps.step(nc.gpsimd.memset(mem.eps[:], EPS))
                steps.step(nc.gpsimd.iota(w["desc_int"][:], pattern=[[-1, 16]], base=16, channel_multiplier=0))
                steps.step(nc.gpsimd.memset(w["nm"][:], 0.0))
                w["built"] = steps.k

            @block.tensor
            def _(pe):
                pe.wait_ge(built, 4)
                pe.wait_ge(loaded, 16 * len(loads))
                for i, (src, dst) in enumerate(turns):
                    if i >= rings:
                        j = i - rings
                        pe.wait_ge((moved_act, moved_dve)[j % 2], j // 2 + 1)
                    if i == from_int:
                        pe.wait_ge(casts, 3)
                    r = src.shape[0]
                    nc.tensor.transpose(psum[i % rings][0:src.shape[1], 0:r], src, mem.ident[0:r, 0:r]).then_inc(turned, 1)
                pe.wait_ge(moved_act, len(turns) // 2)
                pe.wait_ge(moved_dve, len(turns) // 2)
                nc.tensor.matmul(lora[:, 0:3 * P], la_attn[:], lbT_attn[:], start=True, stop=True)
                nc.tensor.matmul(lora[:, 3 * P:4 * P], la_proj[:], lbT_proj[:], start=True, stop=True).then_inc(lora_done, 1)

            @block.scalar
            def _(act):
                for i, (src, dst) in enumerate(turns):
                    if i % 2 == 0:
                        act.wait_ge(turned, i + 1)
                        nc.scalar.copy(dst, psum[i % rings][0:src.shape[1], 0:src.shape[0]]).then_inc(moved_act, 1)

            @block.vector
            def _(dve):
                steps = Chain(dve, Count(chain, 0))
                dve.wait_ge(first, 16)
                for t in range(NT):
                    steps.step(nc.vector.bn_stats(mem.stats[:, t % 2, :], mem.x[:, t, :]))
                    steps.step(nc.vector.bn_aggr(mem.mv[:, t, :], mem.stats[:, t % 2, :]))
                dve.wait_ge(loaded, 16 * len(loads))
                for j in range(3):
                    nc.vector.tensor_scalar(ffn_nat[:, j, :], ffn_int[:, j, :], float(np.float32(1.0 / 127.0)), None,
                                            ALU.mult).then_inc(casts, 1)
                for i, (src, dst) in enumerate(turns):
                    if i % 2 == 1:
                        dve.wait_ge(turned, i + 1)
                        nc.vector.tensor_copy(dst, psum[i % rings][0:src.shape[1], 0:src.shape[0]]).then_inc(moved_dve, 1)
                dve.wait_ge(lora_done, 1)
                dve.wait_ge(moved_act, len(turns) // 2)
                dve.wait_ge(moved_dve, len(turns) // 2)
                for dst, src in ((w["L0_attn_w_attn"][:], lora[:, 0:3 * P]), (w["L0_attn_w_proj"][:], lora[:, 3 * P:4 * P])):
                    steps.step(nc.vector.scalar_tensor_tensor(dst, src, LORA_SCALE, dst, ALU.mult, ALU.add))
                for n in ("L2_attn_Wq", "L2_attn_Wk"):
                    a = w[n][:].rearrange("p (h d) -> p h d", d=HD)
                    r = w[n + "_rot"][:].rearrange("p (h d) -> p h d", d=HD)
                    steps.step(nc.vector.tensor_scalar(r[:, :, 0:HD // 2], a[:, :, HD // 2:HD], -1.0, None, ALU.mult))
                    steps.step(nc.vector.tensor_copy(r[:, :, HD // 2:HD], a[:, :, 0:HD // 2]))
                dve.wait_ge(built, w["built"])
                steps.step(nc.vector.tensor_copy(w["desc"][:], w["desc_int"][:]))
                steps.step(nc.vector.tensor_scalar(w["w_gate"][:], w["w_gate"][:], 0.5, None, ALU.mult))
                steps.step(nc.vector.tensor_scalar(w["b_gate"][:], w["b_gate"][:], 0.5, None, ALU.mult))
                dve.wait_ge(built, w["built"])
                steps.step(nc.vector.tensor_scalar(w["offset"][:], w["offset"][:], 3, None, ALU.bitwise_and))
                steps.step(nc.vector.tensor_scalar(w["same"][:], w["offset"][:], 0.0, BIG, ALU.is_gt, ALU.mult))


def load_last_experts(nc, w, dram):
    loads = [
            (w["L2_ffn_w1"], dram["L2_ffn_w1"].rearrange("e d f -> d e f")),
            (w["L2_ffn_w2"], dram["L2_ffn_w2"].rearrange("e (c f) d -> f e c d", f=P)),
            (w["L3_ffn_gate"][:, 0:8, :], dram["L3_ffn_expert_gate"].rearrange("e d f -> d e f")),
            (w["L3_ffn_gate"][:, 8, :], dram["L3_ffn_shared_gate"]),
            (w["L3_ffn_up"][:, 0:8, :], dram["L3_ffn_expert_up"].rearrange("e d f -> d e f")),
            (w["L3_ffn_up"][:, 8, :], dram["L3_ffn_shared_up"]),
            (w["L3_ffn_down"][:, 0:8, :, :], dram["L3_ffn_expert_down"].rearrange("e (c f) d -> f e c d", f=P)),
            (w["L3_ffn_down"][:, 8, :, :], dram["L3_ffn_shared_down"].rearrange("(c f) d -> f c d", f=P)),
    ]
    with nc.Block() as block:
        @block.sync
        def _(sp):
            for dst, src in loads:
                sp.dma_start(dst, src).then_inc(w["late"], 16)
    w["late_count"] += 16 * len(loads)


def multi_head(nc, mem, w, name, *, wq=None, wq_rot=None, wk=None, wk_rot=None, wv=None, wo, bq=None, bk=None, bv=None,
               bo=None, cross=False, lower=True, mask=None, dram_mask=None, scale=1.0, stick=False, relu=False):
    KEYS = (P, S) if lower else (S, S)
    FIRST = (0, P) if lower else (0, 0)
    AT = (0, S)
    WIDTH = S + S - FIRST[1]
    RING, LAG = 4, 3
    QUADS = H // 4
    rope = wq_rot is not None
    with ExitStack() as ctx:
        sems = ctx.enter_context(Semaphores(nc))

        def sb(n, shape, dt=F32):
            return ctx.enter_context(nc.sbuf_tensor(f"{name}_{n}", shape, dt))

        def ps(n):
            return ctx.enter_context(nc.psum_tensor(f"{name}_{n}", [P, 512], F32))

        def count(n, k=1):
            return Count(sems(f"{name}_{n}"), k)

        h, hT = sb("h", [P, TPB, D]), sb("hT", [P, S])
        cT = sb("cT", [P, S]) if cross else hT
        qT = sb("qT", [P, S]) if wq is not None else hT
        kTm, kT = sb("kTm", [P, H, S]), sb("kT", [P, S])
        turned = sb("roped", [P, 4, S]) if rope else None
        v = sb("v", [P, TPB, H, VW])
        mx = sb("mx", [P, TPB, H])
        nm = w["nm"]
        probs = sb("probs", [P, RING, 2 * S])
        rec, y, yT = sb("rec", [P, TPB, H, 1]), sb("y", [P, TPB, D]), sb("yT", [P, S])
        proj = sb("proj", [P, TPB, D]) if relu else None
        if dram_mask is not None:
            mrow, mcol = sb("mrow", [P, TPB, S]), sb("mcol", [P, TPB * S])
            msum, junk = sb("msum", [P, RING, 2 * S]), sb("junk", [P, TPB, S])
        if stick:
            z, soft = w["scores"][:, 0:H * WIDTH].rearrange("p (h n) -> p h n", h=H), sb("softplus", [P, H, WIDTH])
        psT, psQ, psK, psO = ps("psT"), ps("psQ"), ps("psK"), ps("psO")
        bank = [ps(f"bank{i}") for i in range(RING)]
        O = psO[:, 0:TPB * H * VW].rearrange("p (t h e) -> p t h e", t=TPB, h=H)
        pair = psT[:, 0:S], psT[:, S:2 * S]
        ahead = wq is not None and not rope
        turned_y = psQ[:, S:2 * S] if ahead else pair[1]
        result = psK[:, S:2 * S] if ahead else psK[:, 0:S]

        scales = sems(f"{name}_scales")
        ones_set = sems(f"{name}_v_ones")
        first_chain = sems(f"{name}_first_chain")
        s_h, s_hturned, s_hT, s_cT = count("h_ready"), count("h_turned"), count("hT_ready"), count("cT_ready")
        s_proj, s_q, s_k, s_v = count("projected"), count("q_ready"), count("k_ready", H), count("v_ready")
        s_score, s_max = count("scores_done", H), count("max_done", H)
        s_mturned, s_nm = count("max_turned"), count("neg_max_ready")
        s_logit, s_prob, s_pv = count("logits_done", H), count("probs_ready", H), count("pv_done", H)
        s_y, s_yturned, s_yT, s_out, s_x = (count("y_ready"), count("y_turned"), count("yT_ready"),
                                            count("out_done"), count("x_done"))
        s_mask, s_mt, s_mcol = count("mask_loaded", 16), count("mask_turned"), count("mask_column_ready")
        s_sum = count("masked_logits", H)
        s_z, s_min, s_act, s_ln = count("z_copied", H), count("z_clamped", QUADS), count("exp_done", QUADS), count("ln_done", QUADS)
        s_soft, s_cut = count("softplus_ready", QUADS), count("softplus_masked", QUADS)
        chain = count("dve_chain", 8 + 3 * rope + relu + (wq is not None and not rope))

        layernorm_scales(nc, mem, name, scales)

        with nc.Block() as block:
            if dram_mask is not None:
                @block.sync
                def _(sp):
                    s_mask.credit(sp)
                    with sp.Fori(0, B) as b:
                        sp.wait_ge(s_max.sem, s_max.before(b, H))
                        sp.dma_start(mrow[:], dram_mask[bass.ds(b, 1), 0, :, :].rearrange("a (t p) k -> p (a t) k", p=P)
                                     ).then_inc(s_mask.sem, 16)

            @block.gpsimd
            def _(pool):
                nc.gpsimd.memset(v[:], 1.0).then_inc(ones_set, 1)
                if cross:
                    s_cT.credit(pool)
                    with pool.Fori(0, B) as b:
                        if wk is not None:
                            pool.wait_ge(s_proj.sem, s_proj.before(b, 1))
                        else:
                            pool.wait_ge(s_k.sem, s_k.before(b, H))
                        mem.settle(pool)
                        nc.gpsimd.tensor_copy(cT[:], mem.ctxT[:, bass.ds(b * S, S)]).then_inc(s_cT.sem, 1)
                if stick:
                    s_cut.credit(pool)
                    with pool.Fori(0, B) as b:
                        for c in range(QUADS):
                            pool.wait_ge(s_soft.sem, s_soft.now(b, c + 1))
                            mem.settle(pool)
                            for t in range(TPB):
                                d = soft[:, 4 * c:4 * c + 4, AT[t]:AT[t] + P]
                                last = nc.gpsimd.affine_select(out=d, in_=d, compare_op=ALU.is_gt, fill=0.0, base=0,
                                                               pattern=[[0, 4], [1, P]], channel_multiplier=-1)
                            last.then_inc(s_cut.sem, 1)

            @block.tensor
            def _(pe):
                for c in (s_mt, s_hturned, s_proj, s_score, s_mturned, s_logit, s_pv, s_yturned, s_out):
                    c.credit(pe)

                def project(dst, lhsT, rhs, bias):
                    last = nc.tensor.matmul(dst, lhsT, rhs, start=True, stop=bias is None)
                    if bias is not None:
                        last = nc.tensor.matmul(dst, bias[0], bias[1], start=False, stop=True)
                    return last

                def column_bias(k):
                    return None if k is None else (mem.bias[0:1, k, :], mem.ones_row[0:1, :])

                def row_bias(k):
                    return None if k is None else (mem.ones_row[0:1, 0:P], mem.bias[0:1, k, :])

                def score(g):
                    for t in range(TPB):
                        at = bank[g % RING][:, t * S:t * S + KEYS[t]]
                        masked = mask is not None
                        last = nc.tensor.matmul(at, qT[:, t * P:(t + 1) * P], kTm[:, g, 0:KEYS[t]],
                                                start=True, stop=not masked, skip_group_check=True)
                        if masked:
                            for j, (src, k0, k1) in enumerate(mask[t]):
                                last = nc.tensor.matmul(bank[g % RING][:, t * S + k0:t * S + k1], mem.identb[:], src,
                                                        start=False, stop=j == len(mask[t]) - 1, skip_group_check=True)
                    return last

                def logits(g):
                    for t in range(TPB):
                        n = S - FIRST[t]
                        at = bank[g % RING][:, AT[t]:AT[t] + n]
                        last = nc.tensor.matmul(at, kTm[:, g, t * P:(t + 1) * P], qT[:, FIRST[t]:S],
                                                start=True, stop=stick, skip_group_check=True)
                        if stick:
                            continue
                        last = nc.tensor.matmul(at, w["sel"][:, g, :], nm[:, FIRST[t]:S], start=False, stop=mask is None,
                                                skip_group_check=True)
                        if mask is None:
                            continue
                        parts = [(src[:, t * P - k0:(t + 1) * P - k0], u)
                                 for u in range(TPB) for src, k0, k1 in mask[u] if k0 <= t * P < k1]
                        for j, (m, u) in enumerate(parts):
                            q0 = AT[t] + u * P - FIRST[t]
                            last = nc.tensor.matmul(bank[g % RING][:, q0:q0 + P], m, mem.identb[:], start=False,
                                                    stop=j == len(parts) - 1, skip_group_check=True)
                    return last

                def remains(g):
                    for t in range(TPB):
                        n = S - FIRST[t]
                        at = bank[g % RING][:, AT[t]:AT[t] + n]
                        nc.tensor.matmul(at, kTm[:, g, t * P:(t + 1) * P], qT[:, FIRST[t]:S],
                                         start=True, stop=False, skip_group_check=True)
                        last = nc.tensor.matmul(at, w["neg_tri"][:], soft[:, g, AT[t]:AT[t] + n], start=False, stop=False, skip_group_check=True)
                        if t == 0:
                            nc.tensor.matmul(bank[g % RING][:, P:S], w["neg_ones"][:], soft[:, g, AT[1]:AT[1] + P],
                                             start=False, stop=False, skip_group_check=True)
                        last = nc.tensor.matmul(bank[g % RING][:, AT[t]:AT[t] + P], mem.identb[:], w["strict"][:], start=False,
                                                stop=True, skip_group_check=True)
                    return last

                def weigh(g):
                    for u in range(TPB):
                        tiles = [t for t in range(TPB) if FIRST[t] <= u * P]
                        for j, t in enumerate(tiles):
                            q0 = AT[t] + u * P - FIRST[t]
                            last = nc.tensor.matmul(O[:, u, g, :], probs[:, g % RING, q0:q0 + P], v[:, t, g, :],
                                                    start=j == 0, stop=j == len(tiles) - 1)
                    return last

                def turn(b):
                    pe.wait_ge(s_h.sem, s_h.now(b, 1))
                    mem.settle(pe)
                    for t in range(TPB):
                        last = nc.tensor.transpose(psT[:, t * P:(t + 1) * P], h[:, t, :], mem.ident[:])
                    last.then_inc(s_hturned.sem, 1)

                def projections(b, kept):
                    if cross:
                        pe.wait_ge(s_cT.sem, s_cT.now(b, 1))
                    pe.wait_ge(s_hT.sem, s_hT.now(b, 1))
                    for sem, value in kept:
                        pe.wait_ge(sem, value)
                    mem.settle(pe)
                    project(psQ[:, 0:S], wq, hT[:], column_bias(bq))
                    project(psK[:, 0:S], wk, cT[:], column_bias(bk))
                    if rope:
                        project(psQ[:, S:2 * S], wq_rot, hT[:], None)
                        project(psK[:, S:2 * S], wk_rot, hT[:], None)
                    for t in range(TPB):
                        last = project(psT[:, S + t * P:S + (t + 1) * P], cT[:, t * P:(t + 1) * P], wv, row_bias(bv))
                    last.then_inc(s_proj.sem, 1)

                def batch(b, final):
                    if rope:
                        projections(b, ((s_q.sem, s_q.before(b, 1)), (s_x.sem, s_x.before(b, 1)), (s_yT.sem, s_yT.before(b, 1))))
                    if dram_mask is not None:
                        pe.wait_ge(s_mask.sem, s_mask.now(b, 16))
                        pe.wait_ge(s_mcol.sem, s_mcol.before(b, 1))
                        mem.settle(pe)
                        for t in range(TPB):
                            for u in range(TPB):
                                last = nc.tensor.transpose(psQ[:, t * S + u * P:t * S + (u + 1) * P],
                                                           mrow[:, u, t * P:(t + 1) * P], mem.ident[:])
                        last.then_inc(s_mt.sem, 1)
                    if wq is not None:
                        pe.wait_ge(s_q.sem, s_q.now(b, 1))
                    else:
                        pe.wait_ge(s_hT.sem, s_hT.now(b, 1))
                    if not stick:
                        for g in range(H):
                            pe.wait_ge(s_max.sem, s_max.now(b, g - RING + 1))
                            pe.wait_ge(s_k.sem, s_k.now(b, g + 1))
                            score(g).then_inc(s_score.sem, 1)
                        pe.wait_ge(s_max.sem, s_max.now(b, H))
                        pe.wait_ge(s_hT.sem, s_hT.now(b, 1))
                        mem.settle(pe)
                        for t in range(TPB):
                            last = nc.tensor.transpose(psT[0:H, t * P:(t + 1) * P], mx[:, t, :], mem.ident[:])
                        last.then_inc(s_mturned.sem, 1)
                        pe.wait_ge(s_nm.sem, s_nm.now(b, 1))
                    else:
                        for g in range(H):
                            pe.wait_ge(s_z.sem, s_z.now(b, g - RING + 1))
                            pe.wait_ge(s_k.sem, s_k.now(b, g + 1))
                            logits(g).then_inc(s_logit.sem, 1)
                    pe.wait_ge(s_v.sem, s_v.now(b, 1))
                    pe.wait_ge(s_y.sem, s_y.before(b, 1))
                    for g in range(H + LAG):
                        if g < H and stick:
                            pe.wait_ge(s_cut.sem, s_cut.now(b, g // 4 + 1))
                            pe.wait_ge(s_z.sem, s_z.now(b, min(H, H - RING + g + 1)))
                            pe.wait_ge(s_prob.sem, s_prob.now(b, g - RING + 1))
                            remains(g).then_inc(s_score.sem, 1)
                        elif g < H:
                            pe.wait_ge(s_prob.sem, s_prob.now(b, g - RING + 1))
                            logits(g).then_inc(s_logit.sem, 1)
                        if g >= LAG:
                            pe.wait_ge(s_prob.sem, s_prob.now(b, g - LAG + 1))
                            mem.settle(pe)
                            weigh(g - LAG).then_inc(s_pv.sem, 1)
                    if not final:
                        turn(b + 1)
                        if ahead:
                            projections(b + 1, ((s_k.sem, s_k.now(b, H)), (s_v.sem, s_v.now(b, 1))))
                        else:
                            pe.wait_ge(s_hT.sem, s_hT.now(b + 1, 1))
                    pe.wait_ge(s_y.sem, s_y.now(b, 1))
                    mem.settle(pe)
                    for t in range(TPB):
                        last = nc.tensor.transpose(turned_y[:, t * P:(t + 1) * P], y[:, t, :], mem.ident[:])
                    last.then_inc(s_yturned.sem, 1)
                    pe.wait_ge(s_yT.sem, s_yT.now(b, 1))
                    if not rope:
                        pe.wait_ge(s_x.sem, s_x.before(b, 1))
                    if ahead and not final:
                        pe.wait_ge(s_k.sem, s_k.now(b + 1, 1))
                    mem.settle(pe)
                    for t in range(TPB):
                        last = project(result[:, t * P:(t + 1) * P], yT[:, t * P:(t + 1) * P], wo, row_bias(bo))
                    last.then_inc(s_out.sem, 1)

                turn(0)
                if ahead:
                    projections(0, ())
                each_batch(pe, batch)

            @block.scalar
            def _(act):
                for c in (s_hT, s_yT, s_mcol) + (s_prob,) + ((s_act, s_ln) if stick else ()) + ((s_q,) if wq is not None and not rope else ()):
                    c.credit(act)
                act.preload_act_table_set("natural_log_exp_and_others")

                def keep_h(b):
                    act.wait_ge(s_hturned.sem, s_hturned.now(b, 1))
                    nc.scalar.copy(hT[:], pair[0]).then_inc(s_hT.sem, 1)

                def batch(b, final):
                    if wq is not None and not rope:
                        act.wait_ge(s_proj.sem, s_proj.now(b, 1))
                        act.wait_ge(s_logit.sem, s_logit.before(b, H))
                        if stick:
                            act.wait_ge(s_score.sem, s_score.before(b, H))
                        nc.scalar.mul(qT[:], psQ[:, 0:S], scale if stick else 1.0).then_inc(s_q.sem, 1)
                    if stick:
                        for c in range(QUADS):
                            d = soft[:, 4 * c:4 * c + 4, :]
                            act.wait_ge(s_min.sem, s_min.now(b, c + 1))
                            nc.scalar.activation(d, d, ACT.Exp).then_inc(s_act.sem, 1)
                            act.wait_ge(s_act.sem, s_act.now(b, c + 1))
                            nc.scalar.activation(d, d, ACT.Ln, bias=1.0).then_inc(s_ln.sem, 1)
                    if dram_mask is not None:
                        act.wait_ge(s_mt.sem, s_mt.now(b, 1))
                        act.wait_ge(s_sum.sem, s_sum.before(b, H))
                        nc.scalar.copy(mcol[:], psQ[:]).then_inc(s_mcol.sem, 1)
                    for g in range(H):
                        done = s_score if stick else s_sum if dram_mask is not None else s_logit
                        src = bank[g % RING] if dram_mask is None else msum[:, g % RING, :]
                        act.wait_ge(done.sem, done.now(b, g + 1))
                        act.wait_ge(s_pv.sem, s_pv.now(b, g - RING + 1))
                        nc.scalar.activation(probs[:, g % RING, 0:WIDTH], src[:, 0:WIDTH], ACT.Exp,
                                             scale=1.0 if stick else scale
                                             ).then_inc(s_prob.sem, 1)
                    if not final:
                        if wq is not None:
                            act.wait_ge(s_proj.sem, s_proj.now(b, 1))
                        else:
                            act.wait_ge(s_logit.sem, s_logit.now(b, H))
                        keep_h(b + 1)
                    act.wait_ge(s_yturned.sem, s_yturned.now(b, 1))
                    act.wait_ge(s_out.sem, s_out.before(b, 1))
                    nc.scalar.copy(yT[:], turned_y).then_inc(s_yT.sem, 1)

                keep_h(0)
                each_batch(act, batch)

            @block.vector
            def _(dve):
                for c in (s_h, s_k, s_v, s_y, s_x, s_sum, chain) + ((s_z, s_min, s_soft) if stick else (s_max, s_nm)) + ((s_q,) if rope else ()):
                    c.credit(dve)
                steps = Chain(dve, chain)
                dve.wait_ge(scales, 2)
                dve.wait_ge(ones_set, 1)

                def keys_and_values(b, steps):
                    if wq is not None:
                        dve.wait_ge(s_proj.sem, s_proj.now(b, 1))
                    else:
                        dve.wait_ge(s_cT.sem, s_cT.now(b, 1))
                    dve.wait_ge(s_logit.sem, s_logit.before(b, H))
                    if stick:
                        dve.wait_ge(s_score.sem, s_score.before(b, H))
                    keys = psK[:, 0:S] if wq is not None else cT[:]
                    if rope:
                        table = w["rope"][:]
                        steps.step(nc.vector.tensor_tensor(turned[:, 0:2, :], psQ[:].rearrange("p (a s) -> p a s", a=2), table, ALU.mult))
                        steps.step(nc.vector.tensor_tensor(turned[:, 2:4, :], psK[:].rearrange("p (a s) -> p a s", a=2), table, ALU.mult))
                        nc.vector.tensor_tensor(qT[:], turned[:, 0, :], turned[:, 1, :], ALU.add).then_inc(s_q.sem, 1)
                        steps.step(nc.vector.tensor_tensor(turned[:, 2, :], turned[:, 2, :], turned[:, 3, :], ALU.add))
                        keys = turned[:, 2, :]
                    dve.wait_ge(s_pv.sem, s_pv.before(b, H))
                    source = (pair[1] if wq is not None else tile2(mem.ctx, b))
                    if wq is not None:
                        source = source.rearrange("p (t h e) -> p t h e", t=TPB, h=H)
                    else:
                        mem.settle(dve)
                        source = source.rearrange("p t (h e) -> p t h e", h=H)
                    nc.vector.tensor_copy(v[:, :, :, 0:HD], source).then_inc(s_v.sem, 1)
                    if wq is not None and not rope:
                        steps.step(nc.vector.tensor_copy(kT[:], keys))
                        keys = kT[:]
                    for g in range(H):
                        nc.vector.tensor_scalar(kTm[:, g, :], keys, w["rows"][:, g:g + 1], None, ALU.mult).then_inc(s_k.sem, 1)

                def batch(b, final):
                    steps.batch(b)
                    if stick:
                        for c in range(QUADS + 1):
                            if c < QUADS:
                                for g in range(4 * c, 4 * c + 4):
                                    dve.wait_ge(s_logit.sem, s_logit.now(b, g + 1))
                                    nc.vector.tensor_copy(z[:, g, :], bank[g % RING][:, 0:WIDTH]).then_inc(s_z.sem, 1)
                                dve.wait_ge(s_z.sem, s_z.now(b, 4 * c + 4))
                                nc.vector.tensor_scalar(soft[:, 4 * c:4 * c + 4, :], z[:, 4 * c:4 * c + 4, :], 40.0, None,
                                                        ALU.min).then_inc(s_min.sem, 1)
                            if c > 0:
                                dve.wait_ge(s_ln.sem, s_ln.now(b, c))
                                d = soft[:, 4 * c - 4:4 * c, :]
                                nc.vector.tensor_tensor(d, d, z[:, 4 * c - 4:4 * c, :], ALU.max).then_inc(s_soft.sem, 1)
                    else:
                        dve.wait_ge(s_mturned.sem, s_mturned.before(b, 1))
                        for g in range(H):
                            dve.wait_ge(s_score.sem, s_score.now(b, g + 1))
                            if dram_mask is not None:
                                dve.wait_ge(s_mask.sem, s_mask.now(b, 16))
                                if g:
                                    dve.wait_ge(s_max.sem, s_max.now(b, g))
                                mem.settle(dve)
                                for t in range(TPB):
                                    last = nc.vector.tensor_tensor_reduce(out=junk[:, t, :], in0=bank[g % RING][:, t * S:(t + 1) * S],
                                                                          in1=mrow[:, t, :], scale=1.0, scalar=LEAST, op0=ALU.add,
                                                                          op1=ALU.max, accum_out=mx[:, t, g:g + 1])
                            else:
                                for t in range(TPB):
                                    last = nc.vector.tensor_reduce(mx[:, t, g:g + 1], bank[g % RING][:, t * S:t * S + KEYS[t]],
                                                                   AX.X, ALU.max)
                            last.then_inc(s_max.sem, 1)
                        dve.wait_ge(s_mturned.sem, s_mturned.now(b, 1))
                        steps.step(nc.vector.tensor_scalar(nm[0:H, :], psT[0:H, 0:S], -1.0, None, ALU.mult))
                        nc.vector.scalar_tensor_tensor(nm[32:32 + H, :], psT[0:H, 0:S], -1.0, nm[0:H, :], ALU.mult,
                                                       ALU.subtract).then_inc(s_nm.sem, 1)
                    if dram_mask is not None:
                        dve.wait_ge(s_mcol.sem, s_mcol.now(b, 1))
                        for g in range(H):
                            dve.wait_ge(s_logit.sem, s_logit.now(b, g + 1))
                            dve.wait_ge(s_prob.sem, s_prob.now(b, g - RING + 1))
                            nc.vector.tensor_tensor(msum[:, g % RING, :], bank[g % RING][:], mcol[:], ALU.add).then_inc(s_sum.sem, 1)
                    if not final:
                        dve.wait_ge(s_hturned.sem, s_hturned.now(b, 1))
                        normalize(nc, mem, dve, steps, b + 1, h).then_inc(s_h.sem, 1)
                    dve.wait_ge(s_pv.sem, s_pv.now(b, H))
                    side = y[:].rearrange("p t (h e) -> p t h e", h=H)
                    if stick:
                        steps.step(nc.vector.tensor_scalar(rec[:], O[:, :, :, HD:VW], -1.0, 1.0, ALU.mult, ALU.add))
                        dve.wait_ge(s_yturned.sem, s_yturned.before(b, 1))
                        steps.step(nc.vector.tensor_tensor(side, v[:, :, :, 0:HD], rec[:].to_broadcast([P, TPB, H, HD]), ALU.mult))
                        nc.vector.tensor_tensor(side, side, O[:, :, :, 0:HD], ALU.add).then_inc(s_y.sem, 1)
                    else:
                        steps.step(nc.vector.reciprocal(rec[:], O[:, :, :, HD:VW]))
                        dve.wait_ge(s_yturned.sem, s_yturned.before(b, 1))
                        nc.vector.tensor_tensor(side, O[:, :, :, 0:HD], rec[:].to_broadcast([P, TPB, H, HD]),
                                                ALU.mult).then_inc(s_y.sem, 1)
                    if not final and not rope:
                        keys_and_values(b + 1, steps)
                    dve.wait_ge(s_out.sem, s_out.now(b, 1))
                    add = result.rearrange("p (t d) -> p t d", t=TPB)
                    if relu:
                        steps.step(nc.vector.tensor_scalar(proj[:], add, 0.0, None, ALU.max))
                        add = proj[:]
                    nc.vector.tensor_tensor(tile2(mem.x, b), tile2(mem.x, b), add, ALU.add).then_inc(s_x.sem, 1)
                    if not final and rope:
                        keys_and_values(b + 1, steps)
                    dve.wait_ge(s_x.sem, s_x.now(b, 1))
                    mem.settle(dve)
                    take_stats(nc, mem, dve, steps, b)
                    if not final:
                        steps.done()

                first = Chain(dve, Count(first_chain, 0))
                normalize(nc, mem, dve, first, 0, h).then_inc(s_h.sem, 1)
                keys_and_values(0, first)
                each_batch(dve, batch)


def single_head(nc, mem, w, name, kind):
    gnosis, causal, dilated = kind == "gnosis", kind == "causal", kind == "dilated"
    KEYS = (P, S) if causal else (S, S)
    SC = float(D) ** -0.5
    with ExitStack() as ctx:
        sems = ctx.enter_context(Semaphores(nc))

        def sb(n, shape, dt=F32):
            return ctx.enter_context(nc.sbuf_tensor(f"{name}_{n}", shape, dt))

        def ps(n):
            return ctx.enter_context(nc.psum_tensor(f"{name}_{n}", [P, 512], F32))

        def count(n, k=1):
            return Count(sems(f"{name}_{n}"), k)

        h, hT = sb("h", [P, TPB, D]), sb("hT", [P, S])
        cT = None if dilated else sb("cT", [P, S])
        qT, kT = (sb("qT", [P, S]), sb("kT", [P, S])) if causal else (hT, hT if dilated else cT)
        v = h if dilated else sb("v", [P, TPB, D])
        if gnosis:
            gT, sig, mixed = sb("gT", [GN, 2, S]), sb("tanh", [P, TPB, S]), sb("mixed", [P, TPB, S])
            y, yT = sb("y", [P, TPB, D]), sb("yT", [P, S])
        mx, neg, total, rec = sb("mx", [P, TPB, 1]), sb("neg", [P, TPB]), sb("total", [P, TPB]), sb("rec", [P, TPB])
        e, eT = sb("e", [P, TPB, S]), sb("eT", [P, TPB, S])
        psT, psQ, psV, psS, psG, psE, psO, psY = (ps(n) for n in ("psT", "psQ", "psV", "psS", "psG", "psE", "psO", "psY"))

        scales = sems(f"{name}_scales")
        first_chain = sems(f"{name}_first_chain")
        s_h, s_hturned, s_hT, s_cT, s_vc = (count(n) for n in ("h_ready", "h_turned", "hT_ready", "cT_ready", "v_copied"))
        s_proj, s_kv, s_q = count("projected"), count("v_ready"), count("qk_ready")
        s_score, s_tanh, s_neg, s_exp = count("scores_done"), count("tanh_ready"), count("neg_ready"), count("exp_ready")
        s_eturned, s_eT, s_pv = count("e_turned"), count("eT_ready"), count("pv_done")
        s_y, s_yturned, s_yT, s_out, s_x = (count(n) for n in ("y_ready", "y_turned", "yT_ready", "out_done", "x_done"))
        chain = count("dve_chain", 8 + 2 * gnosis + dilated)

        layernorm_scales(nc, mem, name, scales)

        with nc.Block() as block:
            @block.gpsimd
            def _(pool):
                if not dilated:
                    s_cT.credit(pool)
                    with pool.Fori(0, B) as b:
                        pool.wait_ge(s_score.sem, s_score.before(b, 1))
                        pool.wait_ge(s_proj.sem, s_proj.before(b, 1))
                        mem.settle(pool)
                        nc.gpsimd.tensor_copy(cT[:], mem.ctxT[:, bass.ds(b * S, S)]).then_inc(s_cT.sem, 1)

            @block.tensor
            def _(pe):
                for c in (s_hturned, s_proj, s_score, s_eturned, s_pv, s_yturned, s_out):
                    c.credit(pe)

                def turn(b):
                    pe.wait_ge(s_h.sem, s_h.now(b, 1))
                    pe.wait_ge(s_hT.sem, s_hT.before(b, 1))
                    mem.settle(pe)
                    for t in range(TPB):
                        last = nc.tensor.transpose(psT[:, t * P:(t + 1) * P], h[:, t, :], mem.ident[:])
                    last.then_inc(s_hturned.sem, 1)

                def projections(b):
                    pe.wait_ge(s_hT.sem, s_hT.now(b, 1))
                    pe.wait_ge(s_cT.sem, s_cT.now(b, 1))
                    pe.wait_ge(s_q.sem, s_q.before(b, 1))
                    pe.wait_ge(s_kv.sem, s_kv.before(b, 1))
                    mem.settle(pe)
                    if gnosis:
                        nc.tensor.matmul(psQ[0:GN, 0:S], w["L1_xattn_Wgq"][:], hT[:], start=True, stop=True)
                        nc.tensor.matmul(psQ[0:GN, S:2 * S], w["L1_xattn_Wgk"][:], cT[:], start=True, stop=True
                                         ).then_inc(s_proj.sem, 1)
                    if causal:
                        nc.tensor.matmul(psQ[:, 0:S], w["L2_xattn_Wq"][:], hT[:], start=True, stop=True)
                        nc.tensor.matmul(psQ[:, S:2 * S], w["L2_xattn_Wk"][:], cT[:], start=True, stop=True)
                        for t in range(TPB):
                            last = nc.tensor.matmul(psV[:, t * P:(t + 1) * P], cT[:, t * P:(t + 1) * P],
                                                    w["L2_xattn_Wv"][:], start=True, stop=True)
                        last.then_inc(s_proj.sem, 1)

                def batch(b, final):
                    if dilated:
                        pe.wait_ge(s_hT.sem, s_hT.now(b, 1))
                    if not dilated:
                        pe.wait_ge(s_q.sem, s_q.now(b, 1))
                    pe.wait_ge(s_exp.sem, s_exp.before(b, 1))
                    pe.wait_ge(s_neg.sem, s_neg.before(b, 1))
                    mem.settle(pe)
                    for t in range(TPB):
                        at = psS[:, t * S:t * S + KEYS[t]]
                        last = nc.tensor.matmul(at, qT[:, t * P:(t + 1) * P], kT[:, 0:KEYS[t]], start=True, stop=gnosis,
                                                skip_group_check=True)
                        if causal:
                            last = nc.tensor.matmul(psS[:, t * S + t * P:t * S + (t + 1) * P], mem.identb[:], w["causal"][:],
                                                    start=False, stop=True, skip_group_check=True)
                        if dilated:
                            for u in range(TPB):
                                last = nc.tensor.matmul(psS[:, t * S + u * P:t * S + (u + 1) * P], mem.identb[:], w["same"][:],
                                                        start=False, stop=u == TPB - 1, skip_group_check=True)
                    if gnosis:
                        pe.wait_ge(s_tanh.sem, s_tanh.before(b, 1))
                        mem.settle(pe)
                        for t in range(TPB):
                            last = nc.tensor.matmul(psG[:, t * S:(t + 1) * S], gT[:, 0, t * P:(t + 1) * P], gT[:, 1, :],
                                                    start=True, stop=True)
                    last.then_inc(s_score.sem, 1)
                    if not final and not dilated:
                        turn(b + 1)
                    pe.wait_ge(s_exp.sem, s_exp.now(b, 1))
                    pe.wait_ge(s_eT.sem, s_eT.before(b, 1))
                    mem.settle(pe)
                    for t in range(TPB):
                        for k in range(KEYS[t] // P):
                            last = nc.tensor.transpose(psE[:, k * S + t * P:k * S + (t + 1) * P], e[:, t, k * P:(k + 1) * P],
                                                       mem.ident[:])
                    last.then_inc(s_eturned.sem, 1)
                    if not final and not dilated:
                        projections(b + 1)
                    pe.wait_ge(s_eT.sem, s_eT.now(b, 1))
                    if not dilated:
                        pe.wait_ge(s_kv.sem, s_kv.now(b, 1))
                    if gnosis:
                        pe.wait_ge(s_y.sem, s_y.before(b, 1))
                    else:
                        pe.wait_ge(s_x.sem, s_x.before(b, 1))
                    mem.settle(pe)
                    for t in range(TPB):
                        for k in range(KEYS[t] // P):
                            last = nc.tensor.matmul(psO[:, t * D:(t + 1) * D], eT[:, k, t * P:(t + 1) * P], v[:, k, :],
                                                    start=k == 0, stop=k == KEYS[t] // P - 1)
                    last.then_inc(s_pv.sem, 1)
                    if not final and dilated:
                        turn(b + 1)
                    if gnosis:
                        pe.wait_ge(s_y.sem, s_y.now(b, 1))
                        pe.wait_ge(s_x.sem, s_x.before(b, 1))
                        mem.settle(pe)
                        for t in range(TPB):
                            last = nc.tensor.transpose(psY[:, S + t * P:S + (t + 1) * P], y[:, t, :], mem.ident[:])
                        last.then_inc(s_yturned.sem, 1)
                        pe.wait_ge(s_yT.sem, s_yT.now(b, 1))
                        mem.settle(pe)
                        for t in range(TPB):
                            at = psY[:, t * P:(t + 1) * P]
                            nc.tensor.matmul(at, yT[:, t * P:(t + 1) * P], w["L1_xattn_Wh"][:], start=True, stop=False)
                            last = nc.tensor.matmul(at, mem.ones_row[0:1, 0:P], mem.bias[0:1, BIASES["L1_xattn_bh"], :],
                                                    start=False, stop=True)
                        last.then_inc(s_out.sem, 1)

                turn(0)
                if not dilated:
                    projections(0)
                each_batch(pe, batch)

            @block.scalar
            def _(act):
                mine = (s_hT, s_exp, s_eT) + ((s_q, s_tanh, s_yT) if gnosis else ()) + ((s_q,) if causal else ())
                for c in mine:
                    c.credit(act)
                act.preload_act_table_set("exp_and_others")

                def keep_h(b):
                    act.wait_ge(s_hturned.sem, s_hturned.now(b, 1))
                    act.wait_ge(s_score.sem, s_score.before(b, 1))
                    nc.scalar.copy(hT[:], psT[:, 0:S]).then_inc(s_hT.sem, 1)

                def batch(b, final):
                    if gnosis:
                        act.wait_ge(s_proj.sem, s_proj.now(b, 1))
                        nc.scalar.activation(gT[:, 0, :], psQ[0:GN, 0:S], ACT.Tanh, bias=w["bgq"][:])
                        nc.scalar.activation(gT[:, 1, :], psQ[0:GN, S:2 * S], ACT.Tanh, bias=w["bgk"][:]).then_inc(s_q.sem, 1)
                        act.wait_ge(s_score.sem, s_score.now(b, 1))
                        act.wait_ge(s_neg.sem, s_neg.before(b, 1))
                        nc.scalar.activation(sig[:], psG[:].rearrange("p (t k) -> p t k", t=TPB), ACT.Tanh,
                                             bias=w["b_gate"][:], scale=w["w_gate"][:]).then_inc(s_tanh.sem, 1)
                    if causal:
                        act.wait_ge(s_proj.sem, s_proj.now(b, 1))
                        nc.scalar.copy(qT[:], psQ[:, 0:S])
                        nc.scalar.copy(kT[:], psQ[:, S:2 * S]).then_inc(s_q.sem, 1)
                    act.wait_ge(s_neg.sem, s_neg.now(b, 1))
                    act.wait_ge(s_eturned.sem, s_eturned.before(b, 1))
                    act.wait_ge(s_x.sem, s_x.before(b, 1))
                    for t in range(TPB):
                        src = mixed[:, t, 0:KEYS[t]] if gnosis else psS[:, t * S:t * S + KEYS[t]]
                        last = nc.scalar.activation(e[:, t, 0:KEYS[t]], src, ACT.Exp, bias=neg[:, t:t + 1],
                                                    scale=1.0 if gnosis else SC, accum_out=total[:, t:t + 1])
                    last.then_inc(s_exp.sem, 1)
                    if not final and not dilated:
                        keep_h(b + 1)
                    act.wait_ge(s_eturned.sem, s_eturned.now(b, 1))
                    act.wait_ge(s_pv.sem, s_pv.before(b, 1))
                    if causal:
                        nc.scalar.copy(eT[:, 0, :], psE[:, 0:S])
                        nc.scalar.copy(eT[:, 1, P:S], psE[:, S + P:2 * S]).then_inc(s_eT.sem, 1)
                    else:
                        nc.scalar.copy(eT[:], psE[:].rearrange("p (k q) -> p k q", k=TPB)).then_inc(s_eT.sem, 1)
                    if not final and dilated:
                        keep_h(b + 1)
                    if gnosis:
                        act.wait_ge(s_yturned.sem, s_yturned.now(b, 1))
                        act.wait_ge(s_out.sem, s_out.before(b, 1))
                        nc.scalar.copy(yT[:], psY[:, S:2 * S]).then_inc(s_yT.sem, 1)

                keep_h(0)
                each_batch(act, batch)

            @block.vector
            def _(dve):
                for c in (s_h, s_neg, s_x, chain) + (() if dilated else (s_kv,)) + ((s_y,) if gnosis else ()):
                    c.credit(dve)
                steps = Chain(dve, chain)
                dve.wait_ge(scales, 2)

                def batch(b, final):
                    steps.batch(b)
                    if not dilated:
                        dve.wait_ge(s_pv.sem, s_pv.before(b, 1))
                    if gnosis:
                        mem.settle(dve)
                        nc.vector.tensor_copy(v[:], tile2(mem.ctx, b)).then_inc(s_kv.sem, 1)
                    if causal:
                        dve.wait_ge(s_proj.sem, s_proj.now(b, 1))
                        nc.vector.tensor_copy(v[:], psV[:, 0:S].rearrange("p (t d) -> p t d", t=TPB)).then_inc(s_kv.sem, 1)
                    dve.wait_ge(s_score.sem, s_score.now(b, 1))
                    dve.wait_ge(s_exp.sem, s_exp.before(b, 1))
                    if gnosis:
                        dve.wait_ge(s_tanh.sem, s_tanh.now(b, 1))
                        steps.step(nc.vector.tensor_scalar(sig[:], sig[:], 0.5, 1.5, ALU.mult, ALU.add))
                        steps.step(nc.vector.scalar_tensor_tensor(mixed[:], psS[:].rearrange("p (t k) -> p t k", t=TPB), SC,
                                                                  sig[:], ALU.mult, ALU.mult))
                    for t in range(TPB):
                        src = mixed[:, t, 0:KEYS[t]] if gnosis else psS[:, t * S:t * S + KEYS[t]]
                        last = nc.vector.tensor_reduce(mx[:, t, :], src, AX.X, ALU.max)
                    steps.step(last)
                    nc.vector.tensor_scalar(neg[:], mx[:, :, 0], -1.0 if gnosis else -SC, None, ALU.mult).then_inc(s_neg.sem, 1)
                    if not final and not dilated:
                        dve.wait_ge(s_hturned.sem, s_hturned.now(b, 1))
                        normalize(nc, mem, dve, steps, b + 1, h).then_inc(s_h.sem, 1)
                    dve.wait_ge(s_exp.sem, s_exp.now(b, 1))
                    steps.step(nc.vector.reciprocal(rec[:], total[:]))
                    if dilated:
                        steps.step(nc.vector.tensor_scalar(rec[:], rec[:], 0.25, None, ALU.mult))
                    dve.wait_ge(s_pv.sem, s_pv.now(b, 1))
                    if not final and dilated:
                        dve.wait_ge(s_hturned.sem, s_hturned.now(b, 1))
                        normalize(nc, mem, dve, steps, b + 1, h).then_inc(s_h.sem, 1)
                    if gnosis:
                        dve.wait_ge(s_yturned.sem, s_yturned.before(b, 1))
                        nc.vector.tensor_tensor(y[:], psO[:, 0:S].rearrange("p (t d) -> p t d", t=TPB),
                                                rec[:].unsqueeze(2).to_broadcast([P, TPB, D]), ALU.mult).then_inc(s_y.sem, 1)
                        dve.wait_ge(s_out.sem, s_out.now(b, 1))
                        nc.vector.tensor_tensor(tile2(mem.x, b), tile2(mem.x, b),
                                                psY[:, 0:S].rearrange("p (t d) -> p t d", t=TPB), ALU.add).then_inc(s_x.sem, 1)
                    else:
                        for t in range(TPB):
                            at = mem.x[:, bass.ds(b * TPB + t, 1), :]
                            last = nc.vector.scalar_tensor_tensor(at, psO[:, t * D:(t + 1) * D].unsqueeze(1), rec[:, t:t + 1], at,
                                                                  ALU.mult, ALU.add)
                        last.then_inc(s_x.sem, 1)
                    dve.wait_ge(s_x.sem, s_x.now(b, 1))
                    mem.settle(dve)
                    take_stats(nc, mem, dve, steps, b)
                    if not final:
                        steps.done()

                normalize(nc, mem, dve, Chain(dve, Count(first_chain, 0)), 0, h).then_inc(s_h.sem, 1)
                each_batch(dve, batch)


def back(k, n):
    return k - 2 if k >= 2 else max(j for j in range(n) if j % 2 == k % 2) - n


def normalize_and_turn(nc, mem, w, name, hT, h_all=None, router=None):
    with ExitStack() as ctx:
        sems = ctx.enter_context(Semaphores(nc))

        def sb(n, shape, dt=F32):
            return ctx.enter_context(nc.sbuf_tensor(f"{name}_{n}", shape, dt))

        def count(n, k=1):
            return Count(sems(f"{name}_{n}"), k)

        h, part = sb("h", [P, TPB, D]), sb("hT_part", [P, S])
        psT = ctx.enter_context(nc.psum_tensor(f"{name}_psT", [P, 512], F32))
        psR = ctx.enter_context(nc.psum_tensor(f"{name}_psR", [P, 512], F32))
        scales = sems(f"{name}_scales")
        s_h, s_turned, s_hT, s_all, s_routed, s_logits = (count(n) for n in (
            "h_ready", "h_turned", "hT_ready", "hT_kept", "routed", "logits_kept"))
        chain = count("norm_chain", 1 + (h_all is not None))
        layernorm_scales(nc, mem, name, scales)
        with nc.Block() as block:
            @block.vector
            def _(dve):
                for c in (s_h, chain) + ((s_logits,) if router else ()):
                    c.credit(dve)
                steps = Chain(dve, chain)
                dve.wait_ge(scales, 2)

                def next_h(b):
                    dve.wait_ge(s_turned.sem, s_turned.before(b, 1))
                    normalize(nc, mem, dve, steps, b, h).then_inc(s_h.sem, 1)
                    if h_all is not None:
                        dve.wait_ge(s_h.sem, s_h.now(b, 1))
                        mem.settle(dve)
                        steps.step(nc.vector.tensor_copy(tile2(h_all, b), h[:]))

                def batch(b, final):
                    if not final:
                        steps.batch(b + 1)
                        next_h(b + 1)
                    if router:
                        gate, n, logits = router
                        dve.wait_ge(s_routed.sem, s_routed.now(b, 1))
                        nc.vector.tensor_copy(tile2(logits, b), psR[:, 0:TPB * n].rearrange("p (t e) -> p t e", t=TPB)
                                              ).then_inc(s_logits.sem, 1)

                next_h(0)
                each_batch(dve, batch)

            @block.tensor
            def _(pe):
                for c in (s_turned,) + ((s_routed,) if router else ()):
                    c.credit(pe)

                def turn(b):
                    pe.wait_ge(s_h.sem, s_h.now(b, 1))
                    pe.wait_ge(s_hT.sem, s_hT.before(b, 1))
                    mem.settle(pe)
                    for t in range(TPB):
                        last = nc.tensor.transpose(psT[:, t * P:(t + 1) * P], h[:, t, :], mem.ident[:])
                    last.then_inc(s_turned.sem, 1)

                def batch(b, final):
                    if not final:
                        turn(b + 1)
                    if router:
                        gate, n, logits = router
                        pe.wait_ge(s_hT.sem, s_hT.now(b, 1))
                        pe.wait_ge(s_logits.sem, s_logits.before(b, 1))
                        mem.settle(pe)
                        for t in range(TPB):
                            last = nc.tensor.matmul(psR[:, t * n:(t + 1) * n], part[:, t * P:(t + 1) * P], gate, start=True, stop=True)
                        last.then_inc(s_routed.sem, 1)

                turn(0)
                each_batch(pe, batch)

            @block.scalar
            def _(act):
                for c in (s_hT, s_all):
                    c.credit(act)
                with act.Fori(0, B) as b:
                    act.wait_ge(s_turned.sem, s_turned.now(b, 1))
                    if router:
                        act.wait_ge(s_routed.sem, s_routed.before(b, 1))
                    act.wait_ge(s_all.sem, s_all.before(b, 1))
                    nc.scalar.copy(part[:], psT[:, 0:S]).then_inc(s_hT.sem, 1)
                    act.wait_ge(s_hT.sem, s_hT.now(b, 1))
                    mem.settle(act)
                    nc.scalar.copy(hT[:, bass.ds(b * S, S)], part[:]).then_inc(s_all.sem, 1)


def turn_scaled(nc, mem, w, name, h_all, score, hsT):
    with ExitStack() as ctx:
        sems = ctx.enter_context(Semaphores(nc))

        def count(n, k=1):
            return Count(sems(f"{name}_{n}"), k)

        hs = ctx.enter_context(nc.sbuf_tensor(f"{name}_hs", [P, TPB, D], F32))
        psT = ctx.enter_context(nc.psum_tensor(f"{name}_psX", [P, 512], F32))
        s_hs, s_turned, s_kept = count("scaled"), count("scaled_turned"), count("scaled_kept")
        with nc.Block() as block:
            @block.vector
            def _(dve):
                s_hs.credit(dve)
                with dve.Fori(0, B) as b:
                    dve.wait_ge(s_turned.sem, s_turned.before(b, 1))
                    nc.vector.tensor_tensor(hs[:], tile2(h_all, b), score[:, bass.ds(b * TPB, TPB)].unsqueeze(2).to_broadcast([P, TPB, D]),
                                            ALU.mult).then_inc(s_hs.sem, 1)

            @block.tensor
            def _(pe):
                s_turned.credit(pe)
                with pe.Fori(0, B) as b:
                    pe.wait_ge(s_hs.sem, s_hs.now(b, 1))
                    pe.wait_ge(s_kept.sem, s_kept.before(b, 1))
                    mem.settle(pe)
                    for t in range(TPB):
                        last = nc.tensor.transpose(psT[:, t * P:(t + 1) * P], hs[:, t, :], mem.ident[:])
                    last.then_inc(s_turned.sem, 1)

            @block.scalar
            def _(act):
                s_kept.credit(act)
                with act.Fori(0, B) as b:
                    act.wait_ge(s_turned.sem, s_turned.now(b, 1))
                    mem.settle(act)
                    nc.scalar.copy(hsT[:, bass.ds(b * S, S)], psT[:, 0:S]).then_inc(s_kept.sem, 1)


def experts(nc, mem, w, name, members, func, gates=None, stats=True):
    J = len(members)
    chunks = members[0][3].shape[1]
    groups = [list(range(c, min(c + 2, chunks))) for c in range(0, chunks, 2)]
    units = [(j, g) for j in range(J) for g in groups]
    U, G = len(units), len(groups)
    glu = members[0][2] is not None
    with ExitStack() as ctx:
        sems = ctx.enter_context(Semaphores(nc))

        def sb(n, shape, dt=F32):
            return ctx.enter_context(nc.sbuf_tensor(f"{name}_{n}", shape, dt))

        def ps(n):
            return [ctx.enter_context(nc.psum_tensor(f"{name}_{n}{i}", [P, 512], F32)) for i in range(2)]

        def count(n, k=1):
            return Count(sems(f"{name}_{n}"), k)

        hid = sb("hidden", [P, 2, chunks, S])
        act_out = sb("activated", [P, 2, 2, S]) if glu else None
        psG, psU, psY = ps("psG"), ps("psU") if glu else None, ps("psY")
        n_gates = gates.shape[2] if gates is not None else 1
        gate = sb("gate", [P, TPB, n_gates]) if gates is not None else None
        s_up, s_act, s_hid, s_down, s_add = (count("up_done", U), count("act_done", U), count("hidden_ready", U), count("down_done", J),
                                             count("added", J))
        if not glu:
            s_hid = s_act
        chain = count("dve_chain", 5 * stats + (gates is not None))

        with nc.Block() as block:
            @block.tensor
            def _(pe):
                s_up.credit(pe)
                s_down.credit(pe)
                pe.wait_ge(w["late"], w["late_count"])

                def down(b, j):
                    pe.wait_ge(s_hid.sem, s_hid.now(b, (j + 1) * G))
                    pe.wait_ge(s_add.sem, s_add.now(b, back(j, J) + 1))
                    mem.settle(pe)
                    for t in range(TPB):
                        for c in range(chunks):
                            last = nc.tensor.matmul(psY[j % 2][:, t * D:(t + 1) * D], hid[:, j % 2, c, t * P:(t + 1) * P],
                                                    members[j][3][:, c, :], start=c == 0, stop=c == chunks - 1)
                    last.then_inc(s_down.sem, 1)

                with pe.Fori(0, B) as b:
                    for u, (j, g) in enumerate(units):
                        source, w1, wup, _, _ = members[j]
                        pe.wait_ge(s_hid.sem, s_hid.now(b, back(u, U) + 1))
                        mem.settle(pe)
                        for bank, weight in ((psG, w1), (psU, wup)):
                            if weight is None:
                                continue
                            for i, c in enumerate(g):
                                last = nc.tensor.matmul(bank[u % 2][:, i * S:(i + 1) * S], weight[:, c * P:(c + 1) * P],
                                                        source[:, bass.ds(b * S, S)], start=True, stop=True)
                        last.then_inc(s_up.sem, 1)
                        if g is groups[-1] and j > 0:
                            down(b, j - 1)
                    down(b, J - 1)

            @block.scalar
            def _(act):
                s_act.credit(act)
                act.preload_act_table(func)
                with act.Fori(0, B) as b:
                    for u, (j, g) in enumerate(units):
                        n = len(g)
                        act.wait_ge(s_up.sem, s_up.now(b, u + 1))
                        if glu:
                            act.wait_ge(s_hid.sem, s_hid.now(b, back(u, U) + 1))
                            dst = act_out[:, u % 2, 0:n, :]
                        else:
                            act.wait_ge(s_down.sem, s_down.now(b, back(j, J) + 1))
                            dst = hid[:, j % 2, g[0]:g[0] + n, :]
                        nc.scalar.activation(dst, psG[u % 2][:, 0:n * S].rearrange("p (c s) -> p c s", c=n), func
                                             ).then_inc(s_act.sem, 1)

            @block.vector
            def _(dve):
                for c in (s_add,) + ((chain,) if chain.n else ()) + ((s_hid,) if glu else ()):
                    c.credit(dve)
                steps = Chain(dve, chain)

                def add(b, j):
                    dve.wait_ge(s_down.sem, s_down.now(b, j + 1))
                    dve.wait_ge(s_add.sem, s_add.now(b, j))
                    if members[j][4] is None:
                        last = nc.vector.tensor_tensor(tile2(mem.x, b), tile2(mem.x, b),
                                                       psY[j % 2][:, 0:S].rearrange("p (t d) -> p t d", t=TPB), ALU.add)
                    else:
                        for t in range(TPB):
                            at = mem.x[:, bass.ds(b * TPB + t, 1), :]
                            last = nc.vector.scalar_tensor_tensor(at, psY[j % 2][:, t * D:(t + 1) * D].unsqueeze(1),
                                                                  gate[:, t, members[j][4]:members[j][4] + 1], at, ALU.mult, ALU.add)
                    last.then_inc(s_add.sem, 1)

                with dve.Fori(0, B) as b:
                    steps.batch(b)
                    if gates is not None:
                        dve.wait_ge(s_add.sem, s_add.before(b, J))
                        mem.settle(dve)
                        steps.step(nc.vector.tensor_copy(gate[:], tile2(gates, b)))
                    for u, (j, g) in enumerate(units):
                        n = len(g)
                        if glu:
                            dve.wait_ge(s_act.sem, s_act.now(b, u + 1))
                            dve.wait_ge(s_down.sem, s_down.now(b, back(j, J) + 1))
                            nc.vector.tensor_tensor(hid[:, j % 2, g[0]:g[0] + n, :], act_out[:, u % 2, 0:n, :],
                                                    psU[u % 2][:, 0:n * S].rearrange("p (c s) -> p c s", c=n),
                                                    ALU.mult).then_inc(s_hid.sem, 1)
                        if g is groups[-1] and j > 0:
                            add(b, j - 1)
                    add(b, J - 1)
                    if stats:
                        dve.wait_ge(s_add.sem, s_add.now(b, J))
                        mem.settle(dve)
                        take_stats(nc, mem, dve, steps, b)
                    steps.done()


def route_expert_choice(nc, mem, w, name, logits, gates, E, keep):
    with ExitStack() as ctx:
        sems = ctx.enter_context(Semaphores(nc))

        def sb(n, shape, dt=F32):
            return ctx.enter_context(nc.sbuf_tensor(f"{name}_{n}", shape, dt))

        def sem(n):
            return sems(f"{name}_{n}")

        R = B * E
        mx, total = sb("mx", [P, NT, 1]), sb("total", [P, NT, 1])
        ex, ready = sb("exp", [P, NT, E]), sb("probs", [P, TPB, B, E])
        rows, left = sb("rows", [R, S]), [sb(f"left{i}", [R, S]) for i in range(2)]
        best, chosen = sb("best", [R, 8]), sb("chosen", [R, S])
        psR = ctx.enter_context(nc.psum_tensor(f"{name}_psR", [P, 512], F32))
        psC = ctx.enter_context(nc.psum_tensor(f"{name}_psC", [P, 512], F32))
        chain, e_done, turned, back_turned = sem("chain"), sem("exp_done"), sem("rows_turned"), sem("gates_turned")
        d = {}
        with nc.Block() as block:
            @block.vector
            def _(dve):
                steps = Chain(dve, Count(chain, 0))
                steps.step(nc.vector.tensor_reduce(mx[:], logits[:], AX.X, ALU.max))
                steps.step(nc.vector.tensor_tensor(ex[:], logits[:], mx[:].to_broadcast([P, NT, E]), ALU.subtract))
                d["shifted"] = steps.k
                dve.wait_ge(e_done, 1)
                steps.step(nc.vector.tensor_reduce(total[:], ex[:], AX.X, ALU.add))
                steps.step(nc.vector.reciprocal(total[:], total[:]))
                steps.step(nc.vector.tensor_tensor(ready[:].rearrange("p t b e -> p b t e"), ex[:].rearrange("p (b t) e -> p b t e", t=TPB),
                                                   total[:].rearrange("p (b t) a -> p b t a", t=TPB).to_broadcast([P, B, TPB, E]), ALU.mult))
                d["probs"] = steps.k
                dve.wait_ge(turned, 1)
                steps.step(nc.vector.tensor_copy(rows[:], psR[0:R, 0:S]))
                at = rows
                for i in range(keep // 8):
                    steps.step(nc.vector.max(best[:], at[:]))
                    steps.step(nc.vector.match_replace(left[i % 2][:], best[:], at[:], -1.0))
                    at = left[i % 2]
                steps.step(nc.vector.scalar_tensor_tensor(chosen[:], at[:], 0.0, rows[:], ALU.is_lt, ALU.mult))
                d["chosen"] = steps.k
                dve.wait_ge(back_turned, 1)
                steps.step(nc.vector.tensor_copy(gates[:].rearrange("p (b t) e -> p t b e", t=TPB),
                                                 psC[:, 0:TPB * R].rearrange("p (t b e) -> p t b e", t=TPB, b=B)))

            @block.scalar
            def _(act):
                act.wait_ge(chain, 2)
                nc.scalar.activation(ex[:], ex[:], ACT.Exp).then_inc(e_done, 1)

            @block.tensor
            def _(pe):
                pe.wait_ge(chain, 5)
                for t in range(TPB):
                    last = nc.tensor.transpose(psR[0:R, t * P:(t + 1) * P], ready[:, t, :, :].rearrange("p b e -> p (b e)"), mem.ident[:])
                last.then_inc(turned, 1)
                pe.wait_ge(chain, 7 + 2 * (keep // 8))
                for t in range(TPB):
                    last = nc.tensor.transpose(psC[:, t * R:(t + 1) * R], chosen[:, t * P:(t + 1) * P], mem.ident[0:R, 0:R])
                last.then_inc(back_turned, 1)


def first_best(nc, steps, w, probs, best, equal, key, onehot, n):
    wide = [P, NT, n]
    steps.step(nc.vector.tensor_reduce(best, probs, AX.X, ALU.max))
    steps.step(nc.vector.tensor_tensor(equal, probs, best.to_broadcast(wide), ALU.is_equal))
    desc = w["desc"][:, 0:n].unsqueeze(1).to_broadcast(wide)
    steps.step(nc.vector.tensor_tensor(equal, equal, desc, ALU.mult))
    steps.step(nc.vector.tensor_reduce(key, equal, AX.X, ALU.max))
    steps.step(nc.vector.tensor_tensor(onehot, desc, key.to_broadcast(wide), ALU.is_equal))


def route_top2(nc, mem, w, name, logits, gates, E, capacity):
    with ExitStack() as ctx:
        sems = ctx.enter_context(Semaphores(nc))

        def sb(n, shape, dt=F32):
            return ctx.enter_context(nc.sbuf_tensor(f"{name}_{n}", shape, dt))

        def sem(n):
            return sems(f"{name}_{n}")

        wide = [P, NT, E]
        probs, rest, equal, count = sb("probs", wide), sb("rest", wide), sb("equal", wide), sb("count", wide)
        one = [sb(f"onehot{i}", wide) for i in range(2)]
        val = [sb(f"val{i}", [P, NT, 1]) for i in range(2)]
        key, total = sb("key", [P, NT, 1]), sb("total", [P, NT, 1])
        ahead = sb("ahead", [P, NT, E])
        psR = ctx.enter_context(nc.psum_tensor(f"{name}_psR", [P, 2, NT, E], F32))
        chain, e_done, ranked = sem("chain"), sem("exp_done"), sem("ranked")
        with nc.Block() as block:
            @block.scalar
            def _(act):
                nc.scalar.activation(probs[:], logits[:], ACT.Exp, scale=-1.0).then_inc(e_done, 1)

            @block.tensor
            def _(pe):
                pe.wait_ge(chain, 14)
                nc.tensor.matmul(psR[:, 0, :, :], w["earlier"][:], count[:], start=True, stop=True)
                nc.tensor.matmul(psR[:, 1, :, :], w["ones"][:], count[:], start=True, stop=True).then_inc(ranked, 1)

            @block.vector
            def _(dve):
                steps = Chain(dve, Count(chain, 0))
                dve.wait_ge(e_done, 1)
                steps.step(nc.vector.tensor_scalar(probs[:], probs[:], 1.0, None, ALU.add))
                steps.step(nc.vector.reciprocal(probs[:], probs[:]))
                first_best(nc, steps, w, probs[:], val[0][:], equal[:], key[:], one[0][:], E)
                steps.step(nc.vector.scalar_tensor_tensor(rest[:], one[0][:], -2.0, probs[:], ALU.mult, ALU.add))
                first_best(nc, steps, w, rest[:], val[1][:], equal[:], key[:], one[1][:], E)
                steps.step(nc.vector.tensor_tensor(count[:], one[0][:], one[1][:], ALU.add))
                assert steps.k == 14
                steps.step(nc.vector.tensor_tensor(total[:], val[0][:], val[1][:], ALU.add))
                steps.step(nc.vector.tensor_scalar(total[:], total[:], 1e-6, None, ALU.add))
                steps.step(nc.vector.reciprocal(total[:], total[:]))
                for i in range(2):
                    steps.step(nc.vector.tensor_tensor(val[i][:], val[i][:], total[:], ALU.mult))
                    steps.step(nc.vector.tensor_tensor(one[i][:], one[i][:], val[i][:].to_broadcast(wide), ALU.mult))
                steps.step(nc.vector.tensor_tensor(one[0][:], one[0][:], one[1][:], ALU.add))
                dve.wait_ge(ranked, 1)
                steps.step(nc.vector.memset(ahead[:], 0.0))
                for t in range(1, NT):
                    steps.step(nc.vector.tensor_tensor(ahead[:, t, :], ahead[:, t - 1, :], psR[:, 1, t - 1, :], ALU.add))
                steps.step(nc.vector.tensor_tensor(ahead[:], ahead[:], psR[:, 0, :, :], ALU.add))
                steps.step(nc.vector.scalar_tensor_tensor(gates[:], ahead[:], float(capacity) - 0.5, one[0][:], ALU.is_lt, ALU.mult))


def route_top1(nc, mem, w, name, logits, gates, score, E):
    with ExitStack() as ctx:
        sems = ctx.enter_context(Semaphores(nc))

        def sb(n, shape, dt=F32):
            return ctx.enter_context(nc.sbuf_tensor(f"{name}_{n}", shape, dt))

        def sem(n):
            return sems(f"{name}_{n}")

        top, key, equal = sb("top", [P, NT, 1]), sb("key", [P, NT, 1]), sb("equal", [P, NT, E])
        chain, e_done = sem("chain"), sem("exp_done")
        with nc.Block() as block:
            @block.vector
            def _(dve):
                steps = Chain(dve, Count(chain, 0))
                first_best(nc, steps, w, logits[:], top[:], equal[:], key[:], gates[:], E)
                dve.wait_ge(e_done, 1)
                steps.step(nc.vector.tensor_scalar(score[:], score[:], 1.0, None, ALU.add))
                steps.step(nc.vector.reciprocal(score[:], score[:]))

            @block.scalar
            def _(act):
                act.wait_ge(chain, 1)
                nc.scalar.activation(score[:], top[:, :, 0], ACT.Exp, scale=-1.0).then_inc(e_done, 1)


def decoder(nc, dram, out):
    with ExitStack() as ctx:
        def sb(name, shape, dt=F32):
            return ctx.enter_context(nc.sbuf_tensor(name, shape, dt))

        mem = Mem(nc, ctx)
        w = {n: sb("wT_" + n, [P, P]) for n in SQUARE + DIRECT}
        w["L0_attn_w_attn"] = sb("wT_L0_attn", [P, 3 * P])
        w["L2_attn_Wq_rot"], w["L2_attn_Wk_rot"] = sb("wT_L2_q_rot", [P, P]), sb("wT_L2_k_rot", [P, P])
        w["L0_ffn_w_gate"], w["L0_ffn_w_up"] = sb("wT_L0_gate", [P, HID0]), sb("wT_L0_up", [P, HID0])
        w["L0_ffn_w_down"] = sb("wT_L0_down", [P, 3, P])
        w["L1_xattn_Wgq"], w["L1_xattn_Wgk"] = sb("wT_L1_gq", [P, GN]), sb("wT_L1_gk", [P, GN])
        w["bgq"], w["bgk"] = sb("bgq", [GN, 1]), sb("bgk", [GN, 1])
        w["w_gate"], w["b_gate"] = sb("w_gate", [P, 1]), sb("b_gate", [P, 1])
        w["rope"] = sb("rope_cos_sin", [P, 2, S])
        w["L1_ffn_gate_w"], w["L2_ffn_gate_w"], w["L3_ffn_router_w"] = sb("wT_r1", [P, 8]), sb("wT_r2", [P, 16]), sb("wT_r3", [P, 8])
        shared = sb("experts_L1_L3", [P, 8 * 512 + 8 * 4 * P])
        w["L1_ffn_w1"] = shared[:, 0:8 * 512].rearrange("p (e f) -> p e f", e=8)
        w["L1_ffn_w2"] = shared[:, 8 * 512:].rearrange("p (e c d) -> p e c d", e=8, c=4)
        w["scores"] = sb("scores_L1_experts_L2", [P, 16 * 256 + 16 * 2 * P])
        w["L2_ffn_w1"] = w["scores"][:, 0:16 * 256].rearrange("p (e f) -> p e f", e=16)
        w["L2_ffn_w2"] = w["scores"][:, 16 * 256:].rearrange("p (e c d) -> p e c d", e=16, c=2)
        w["L3_ffn_gate"], w["L3_ffn_up"] = (shared[:, i * 9 * 256:(i + 1) * 9 * 256].rearrange("p (e f) -> p e f", e=9) for i in range(2))
        w["L3_ffn_down"] = shared[:, 2 * 9 * 256:3 * 9 * 256].rearrange("p (e c d) -> p e c d", e=9, c=2)
        w["causal"], w["same"], w["trinity"] = sb("causal", [P, P], BF16), sb("same", [P, P], BF16), sb("trinity", [P, TPB, S], BF16)
        w["strict"] = sb("strict", [P, P], BF16)
        w["offset"] = sb("offset", [P, P], I32)
        w["sel"], w["nm"] = sb("sel", [P, H, P], BF16), sb("neg_max", [P, S], BF16)
        w["rows"] = sb("head_rows", [P, H])
        w["neg_tri"], w["neg_ones"], w["ones"], w["earlier"] = (sb(n, [P, P]) for n in ("neg_tri", "neg_ones", "ones", "earlier"))
        w["desc"], w["desc_int"] = sb("desc", [P, 16]), sb("desc_int", [P, 16], I32)
        w["late"] = ctx.enter_context(nc.semaphore("experts_loaded"))
        load_and_turn(nc, mem, w, dram)

        causal = [[(w["causal"][:], 0, P)], [(w["causal"][:], P, S)]]
        trinity = [[(w["trinity"][:, 0, 0:P], 0, P)], [(w["trinity"][:, 1, :], 0, S)]]
        qk = float(HD) ** -0.5
        W0 = w["L0_attn_w_attn"]
        multi_head(nc, mem, w, "L0a", wq=W0[:, 0:P], wk=W0[:, P:2 * P], wv=W0[:, 2 * P:3 * P], wo=w["L0_attn_w_proj"][:],
                   bq=0, bk=1, bv=2, bo=3, mask=causal, scale=qk)
        multi_head(nc, mem, w, "L0x", wq=w["L0_xattn_Wq"][:], wk=w["L0_xattn_Wk"][:], wv=w["L0_xattn_Wv"][:],
                   wo=w["L0_xattn_Wo"][:], bq=4, bk=5, bv=6, bo=7, cross=True, mask=trinity, scale=qk)
        with nc.sbuf_tensor("hT0", [P, NT * P], F32) as hT:
            normalize_and_turn(nc, mem, w, "L0n", hT)
            experts(nc, mem, w, "L0f", [(hT, w["L0_ffn_w_gate"][:], w["L0_ffn_w_up"][:], w["L0_ffn_w_down"][:], None)], ACT.Silu)

        multi_head(nc, mem, w, "L1a", wq=w["L1_attn_Wq"][:], wk=w["L1_attn_Wk"][:], wv=w["L1_attn_Wv"][:],
                   wo=w["L1_attn_Wo"][:], scale=qk, stick=True)
        single_head(nc, mem, w, "L1x", "gnosis")
        with nc.sbuf_tensor("hT1", [P, NT * P], F32) as hT, nc.sbuf_tensor("logits1", [P, NT, 8], F32) as logits, \
                nc.sbuf_tensor("gates1", [P, NT, 8], F32) as gates:
            normalize_and_turn(nc, mem, w, "L1n", hT, router=(w["L1_ffn_gate_w"][:], 8, logits))
            route_expert_choice(nc, mem, w, "L1r", logits, gates, 8, int(2.0 * S / 8))
            experts(nc, mem, w, "L1f", [(hT, w["L1_ffn_w1"][:, e, :], None, w["L1_ffn_w2"][:, e, :, :], e) for e in range(8)],
                    ACT.Gelu, gates)
        load_last_experts(nc, w, dram)

        multi_head(nc, mem, w, "L2a", wq=w["L2_attn_Wq"][:], wq_rot=w["L2_attn_Wq_rot"][:], wk=w["L2_attn_Wk"][:],
                   wk_rot=w["L2_attn_Wk_rot"][:], wv=w["L2_attn_Wv"][:], wo=w["L2_attn_Wo"][:], mask=causal, scale=qk)
        single_head(nc, mem, w, "L2x", "causal")
        with nc.sbuf_tensor("hT2", [P, NT * P], F32) as hT, nc.sbuf_tensor("logits2", [P, NT, 16], F32) as logits, \
                nc.sbuf_tensor("gates2", [P, NT, 16], F32) as gates:
            normalize_and_turn(nc, mem, w, "L2n", hT, router=(w["L2_ffn_gate_w"][:], 16, logits))
            route_top2(nc, mem, w, "L2r", logits, gates, 16, int(1.25 * B * S * 2 / 16))
            experts(nc, mem, w, "L2f", [(hT, w["L2_ffn_w1"][:, e, :], None, w["L2_ffn_w2"][:, e, :, :], e) for e in range(16)],
                    ACT.Gelu, gates)

        single_head(nc, mem, w, "L3a", "dilated")
        multi_head(nc, mem, w, "L3x", wo=w["L3_xattn_wo_w"][:], bo=9, cross=True, lower=False,
                   dram_mask=dram["mask_Bx1xSxS2_ff0"], scale=1.0, relu=True)
        with nc.sbuf_tensor("hT3", [P, NT * P], F32) as hT, nc.sbuf_tensor("hsT3", [P, NT * P], F32) as hsT, \
                nc.sbuf_tensor("h3", [P, NT, D], F32) as h_all, nc.sbuf_tensor("logits3", [P, NT, 8], F32) as logits, \
                nc.sbuf_tensor("gates3", [P, NT, 8], F32) as gates, nc.sbuf_tensor("score3", [P, NT], F32) as score:
            normalize_and_turn(nc, mem, w, "L3n", hT, h_all, router=(w["L3_ffn_router_w"][:], 8, logits))
            route_top1(nc, mem, w, "L3r", logits, gates, score, 8)
            turn_scaled(nc, mem, w, "L3s", h_all, score, hsT)
            members = [(hsT, w["L3_ffn_gate"][:, e, :], w["L3_ffn_up"][:, e, :], w["L3_ffn_down"][:, e, :, :], e) for e in range(8)]
            members += [(hT, w["L3_ffn_gate"][:, 8, :], w["L3_ffn_up"][:, 8, :], w["L3_ffn_down"][:, 8, :, :], None)]
            experts(nc, mem, w, "L3f", members, ACT.Silu, gates, stats=False)

        stored = ctx.enter_context(nc.semaphore("stored"))
        with nc.Block() as block:
            @block.sync
            def _(sp):
                sp.dma_start(out.rearrange("b (t p) d -> p (b t) d", p=P), mem.x[:]).then_inc(stored, 16)
                sp.wait_ge(stored, 16)


_INS = ["x", "ctx_1024", "mask_Bx1xSxS2_ff0", "L0_attn_w_attn", "L0_attn_b_attn", "L0_attn_la_attn", "L0_attn_lb_attn",
        "L0_attn_w_proj", "L0_attn_b_proj", "L0_attn_la_proj", "L0_attn_lb_proj", "L0_xattn_Wq", "L0_xattn_bq",
        "L0_xattn_Wk", "L0_xattn_bk", "L0_xattn_Wv", "L0_xattn_bv", "L0_xattn_Wo", "L0_xattn_bo", "L0_ffn_w_gate",
        "L0_ffn_w_up", "L0_ffn_w_down", "L1_attn_Wq", "L1_attn_Wk", "L1_attn_Wv", "L1_attn_Wo", "L1_xattn_Wgq",
        "L1_xattn_bgq", "L1_xattn_Wgk", "L1_xattn_bgk", "L1_xattn_w_gate", "L1_xattn_b_gate", "L1_xattn_Wh",
        "L1_xattn_bh", "L1_ffn_gate_w", "L1_ffn_w1", "L1_ffn_w2", "L2_attn_Wq", "L2_attn_Wk", "L2_attn_Wv", "L2_attn_Wo",
        "L2_xattn_Wq", "L2_xattn_Wk", "L2_xattn_Wv", "L2_ffn_gate_w", "L2_ffn_w1", "L2_ffn_w2", "L3_xattn_wo_w",
        "L3_xattn_wo_b", "L3_ffn_router_w", "L3_ffn_expert_gate", "L3_ffn_expert_up", "L3_ffn_expert_down",
        "L3_ffn_shared_gate", "L3_ffn_shared_up", "L3_ffn_shared_down"]
ROPE_BASE = 10000.0


def rope_table():
    inv = (1.0 / ROPE_BASE ** (np.arange(0, HD, 2, dtype=np.float32) / HD)).astype(np.float32)
    angle = np.outer(np.arange(S, dtype=np.float32), inv).astype(np.float32)
    angle = np.concatenate([angle, angle], axis=1).T
    one = np.stack([np.cos(angle), np.sin(angle)], axis=1)
    return np.ascontiguousarray(np.tile(one, (H, 1, 1)).astype(np.float32))


def kernel(**inputs):
    import concourse.bacc as _bacc
    from concourse.bass_utils import run_bass_kernel_spmd as _run

    nc = _bacc.Bacc("TRN2", target_bir_lowering=False, num_devices=1)
    arrays, dram = {}, {}
    for name in _INS + ["rope"]:
        a = rope_table() if name == "rope" else np.ascontiguousarray(inputs[name])
        if a.ndim == 0:
            a = a.reshape(1)
        arrays[f"in_{name}_dram"] = a
        dram[name] = nc.dram_tensor(f"in_{name}_dram", a.shape, mybir.dt.from_np(a.dtype), kind="ExternalInput").ap()
    out = nc.dram_tensor("out_0_dram", (B, S, D), F32, kind="ExternalOutput").ap()
    decoder(nc, dram, out)
    r = _run(nc, [arrays], core_ids=[0])
    return r.results[0]["out_0_dram"]
```
